# Optimizing a Trainium2 kernel written in Bass

```python
import numpy as np
import jax
import jax.numpy as jnp

def _softmax(x, axis=-1):
    return jax.nn.softmax(x, axis=axis)
def _gelu(x):
    return jax.nn.gelu(x, approximate=True)
def _silu(x):
    return jax.nn.silu(x)
def _sigmoid(x):
    return jax.nn.sigmoid(x)
def _layernorm(x, axis=-1, eps=1e-5):
    m = jnp.mean(x, axis=axis, keepdims=True)
    v = jnp.var(x, axis=axis, keepdims=True)
    return (x - m) / jnp.sqrt(v + eps)
def _scatter_add(tgt, idx, src, axis=0):
    return tgt.at[idx].add(src)
def _segment_sum(src, seg, n):
    return jax.ops.segment_sum(src, seg, n)

kernel_name = 'mk_adj_preln_d2_adj_256_de66d6'

def setup_inputs(seed: int = 0):
    np.random.seed(seed)
    _w = jnp.asarray
    def _rec_inputs():
        import jax
        import jax.numpy as jnp
        _gk = jax.random.key(seed)
        x = -0.0005146 + 1 * jax.random.normal(jax.random.fold_in(_gk, 1), (8, 2048, 256), jnp.float32)
        _w = (1.0 + jnp.arange(2048, dtype=jnp.float32)) ** -0.5
        _w = _w / _w.mean()
        _pij = jnp.clip(0.015625 * _w[:, None] * _w[None, :], 0.0, 1.0)
        _a = jax.random.uniform(jax.random.fold_in(_gk, 2), (8, 2048, 2048)) < _pij
        adj = _a.astype(jnp.int32)
        return x, adj
    x, adj = _rec_inputs()
    def _L0_gnn_setup():
        import jax, jax.numpy as jnp
        import numpy as np
        B, N, C, OUT, S = (4, 2048, 256, 256, 25)
        DENSITY = 0.008
        key = jax.random.key(seed)
        kA, kX, kW = jax.random.split(key, 3)
        A = jax.random.bernoulli(kA, DENSITY, (B, N, N)).astype(jnp.int32)
        X = jax.random.normal(kX, (B, N, C), dtype=jnp.float32)
        W = jax.random.normal(kW, (2 * C, OUT), dtype=jnp.float32) * np.float32(1.0 / np.sqrt(2 * C))
        b = jnp.zeros((OUT,), dtype=jnp.float32)
        return {'A': A, 'X': X, 'W': W, 'b': b}
    _L0_gnn_all = _L0_gnn_setup()
    _L0_gnn_in = {k: v for k, v in _L0_gnn_all.items() if k in ('W', 'b', )}
    del _L0_gnn_all

    def _L1_gnn_setup():
        import jax, jax.numpy as jnp
        import numpy as np
        NEG_BIG = -9000000000000000.0
        ALPHA = 0.2
        key = jax.random.key(seed)
        k1, k2, k3, k4 = jax.random.split(key, 4)
        B, N, Fin, Fout = (8, 2048, 256, 256)
        h = jax.random.normal(k1, (B, N, Fin), dtype=jnp.float32)
        adj = jax.random.randint(k2, (B, N, N), 0, 2, dtype=jnp.int32)
        limW = 1.414 * np.sqrt(6.0 / (Fin + Fout))
        W = jax.random.uniform(k3, (Fin, Fout), jnp.float32, -limW, limW)
        lima = 1.414 * np.sqrt(6.0 / (2 * Fout + 1))
        a = jax.random.uniform(k4, (2 * Fout, 1), jnp.float32, -lima, lima)
        return {'h': h, 'adj': adj, 'W': W, 'a': a}
    _L1_gnn_all = _L1_gnn_setup()
    _L1_gnn_in = {k: v for k, v in _L1_gnn_all.items() if k in ('W', 'a', )}
    del _L1_gnn_all

    return {
        "x": x,
        "adj": adj,
        "L0_gnn_W": _L0_gnn_in["W"],
        "L0_gnn_b": _L0_gnn_in["b"],
        "L1_gnn_W": _L1_gnn_in["W"],
        "L1_gnn_a": _L1_gnn_in["a"],
    }

def reference(x, adj, L0_gnn_W, L0_gnn_b, L1_gnn_W, L1_gnn_a):
    import jax
    import jax.numpy as jnp
    def _L0_gnn_ref(A, X, W, b):
        import jax, jax.numpy as jnp
        import numpy as np
        B, N, C, OUT, S = (4, 2048, 256, 256, 25)
        DENSITY = 0.008
        mask = A != 0
        neg_inf = jnp.float32(-jnp.inf)
        pri = -jnp.arange(N, dtype=jnp.float32)
        scores = jnp.where(mask, pri, neg_inf)
        vals, idx = jax.lax.top_k(scores, S)
        valid = vals > neg_inf
        feats = jax.vmap(lambda x, i: x[i])(X, idx)
        feats = jnp.where(valid[..., None], feats, neg_inf)
        agg = feats.max(axis=2)
        degree = mask.sum(axis=-1)
        agg = jnp.where((degree <= S)[..., None], jnp.maximum(agg, 0.0), agg)
        h = jnp.concatenate([X, agg], axis=-1)
        out = jax.nn.relu(jnp.einsum('bnf,fo->bno', h, W) + b)
        return out

    def _L1_gnn_ref(h, adj, W, a):
        import jax, jax.numpy as jnp
        import numpy as np
        NEG_BIG = -9000000000000000.0
        ALPHA = 0.2
        Fout = W.shape[1]
        wh = jnp.einsum('bni,io->bno', h, W)
        a1 = a[:Fout, 0]
        a2 = a[Fout:, 0]
        s1 = wh @ a1
        s2 = wh @ a2
        e = jax.nn.leaky_relu(s1[:, :, None] + s2[:, None, :], negative_slope=ALPHA)
        e = jnp.where(adj > 0, e, NEG_BIG)
        attention = jax.nn.softmax(e, axis=2)
        h_prime = jnp.einsum('bmn,bno->bmo', attention, wh)
        return h_prime

    h = jnp.maximum(_layernorm(x, axis=-1), 0.0)
    x = x + _L0_gnn_ref(adj, h, L0_gnn_W, L0_gnn_b)
    h = jnp.maximum(_layernorm(x, axis=-1), 0.0)
    x = x + _L1_gnn_ref(h, adj, L1_gnn_W, L1_gnn_a)
    return x


_drawn_inputs = setup_inputs


def setup_inputs(seed=0):
    import zlib

    import numpy as np

    out = dict(_drawn_inputs(seed))
    spreads = {'L0_gnn_b': (0.0, 0.1)}
    factors = {}
    for name, (base, spread) in spreads.items():
        noise = np.random.default_rng([zlib.crc32(name.encode()), seed]).standard_normal(out[name].shape)
        drawn = base * np.exp(spread * noise) if base else spread * noise
        out[name] = jnp.asarray(drawn.astype(out[name].dtype))
    for name, factor in factors.items():
        out[name] = (out[name] * factor).astype(out[name].dtype)
    return out
```

```python
from contextlib import ExitStack

import concourse.bass as bass
from concourse import mybir

P = 128
GRAPHS, NODES, CH = 8, 2048, 256
PICKS = 25
TILES_PER_GRAPH = NODES // P
TILES = GRAPHS * TILES_PER_GRAPH
TABLE_ROWS = NODES + 1
TABLE_GRAPHS = 3
ROUNDS = (PICKS + 7) // 8
NORM_LEAD, UPDATE_LAG, ATTEND_LAG = 18, 2, 18
LN_EPS = 1e-5
NEWTON_STEPS = 3
ROOT_GUESS = 0x5F3759DF
LN_OPS = 4 + 3 * NEWTON_STEPS
LEAKY_SLOPE = 0.2
NEG_BIG = -9e15
CHUNKS = NODES // 512

PHASES = [
    (-NORM_LEAD, 2 - NORM_LEAD, "n"),
    (2 - NORM_LEAD, TILES_PER_GRAPH - NORM_LEAD, "n"),
    (TILES_PER_GRAPH - NORM_LEAD, 0, "n"),
    (0, UPDATE_LAG, "np"),
    (UPDATE_LAG, UPDATE_LAG + 2, "npu"),
    (UPDATE_LAG + 2, ATTEND_LAG, "npu"),
    (ATTEND_LAG, ATTEND_LAG + 2, "npua"),
    (ATTEND_LAG + 2, TILES - NORM_LEAD, "npua"),
    (TILES - NORM_LEAD, TILES, "pua"),
    (TILES, TILES + UPDATE_LAG, "ua"),
    (TILES + UPDATE_LAG, TILES + ATTEND_LAG, "a"),
]


def run_steps(eng, body):
    for first, end, stages in PHASES:
        if end - first == 2:
            body(first, 0, stages)
            body(first, 1, stages)
            continue
        with eng.Fori(0, (end - first) // 2) as pair:
            body(pair * 2 + first, 0, stages)
            body(pair * 2 + first, 1, stages)


def wait(eng, sem, count):
    if not isinstance(count, int) or count > 0:
        eng.wait_ge(sem, count)


def hold(eng, sem, count):
    eng.wait_ge(sem, count)
    eng.nop(nofuse=True)


def graph_layers(nc, x, adj, w0, b0, w1, a1, out):
    fp32, bf16, fp16 = mybir.dt.float32, mybir.dt.bfloat16, mybir.dt.float16
    i32, u32 = mybir.dt.int32, mybir.dt.uint32
    ALU = mybir.AluOpType
    ACT = mybir.ActivationFunctionType
    AX = mybir.AxisListType

    x_rows = x.rearrange("g n c -> (g n) c")
    adj_rows = adj.rearrange("g n m -> (g n) m")
    out_rows = out.rearrange("g n c -> (g n) c")
    table = nc.dram_tensor("table", [TABLE_GRAPHS * TABLE_ROWS, CH], fp32, kind="Internal").ap()
    x1_rows = nc.dram_tensor("x1_rows", [GRAPHS * NODES, CH], fp32, kind="Internal").ap()

    def tile_rows(rows, tile):
        return rows[bass.ds(tile * P, P), :]

    def table_tile(tile):
        graph_slot = tile // TILES_PER_GRAPH % TABLE_GRAPHS
        return table[bass.ds(graph_slot * TABLE_ROWS + tile % TILES_PER_GRAPH * P, P), :]

    ZERO_RUN = (TABLE_GRAPHS - 1) * TABLE_ROWS * CH // P

    with ExitStack() as ctx:
        def sb(name, shape, dt=fp32):
            return ctx.enter_context(nc.sbuf_tensor(name, shape, dt))

        def ps(name, shape, dt=fp32):
            return ctx.enter_context(nc.psum_tensor(name, shape, dt))

        def sem(name):
            return ctx.enter_context(nc.semaphore(name))

        def sem2(name):
            return [sem(f"{name}{i}") for i in range(2)]

        ident_zero = sb("ident_zero", [P, P])
        ident = sb("ident", [P, P])
        ones = sb("ones", [P, P])
        countdown = sb("countdown", [P, NODES], fp16)
        w0_sb = sb("w0_sb", [P, 4, CH])
        b0_sb = sb("b0_sb", [1, CH])
        w1s = sb("w1s", [P, 2, CH + 1])
        a_bc = sb("a_bc", [P, 2 * CH])
        a_prod = sb("a_prod", [P, CH])
        wa = sb("wa", [P, 4])
        w2_bc = sb("w2_bc", [P, 2, P])
        table_base = sb("table_base", [P, 9])
        table_base_i = sb("table_base_i", [P, 9], i32)
        x_norm = sb("x_norm", [P, 2, CH])
        h_out = sb("h_out", [P, 2, CH])
        ln_stats = sb("ln_stats", [P, 2, 6])
        ln_mv = sb("ln_mv", [P, 2, 2])
        ln_var = sb("ln_var", [P, 2])
        ln_root = sb("ln_root", [P, 2])
        ln_err = sb("ln_err", [P, 2])
        ln_scale = sb("ln_scale", [P, 2, 2])
        ln_shift = sb("ln_shift", [P, 2, 2])
        adj_pick = sb("adj_pick", [P, NODES], i32)
        keys = sb("keys", [P, 2, NODES], fp16)
        top = sb("top", [P, 8 * ROUNDS], fp16)
        picks = sb("picks", [P, 2, PICKS], u32)
        rows = sb("rows", [P, 2, PICKS * CH])
        x_upd = sb("x_upd", [P, 2, CH])
        h_upd = sb("h_upd", [P, 2, CH])
        agg = sb("agg", [P, CH])
        ha_t = sb("ha_t", [P, 4, P])
        x1 = sb("x1", [P, 2, CH])
        h2 = sb("h2", [P, CH])
        h2_t = sb("h2_t", [P, 2, P])
        wh = sb("wh", [P, 2 * TILES_PER_GRAPH, CH + 1])
        s1 = sb("s1", [P, 2 * TILES_PER_GRAPH])
        s2 = sb("s2", [P, 2 * NODES])
        adj_att = sb("adj_att", [P, NODES], i32)
        off_mask = sb("off_mask", [P, NODES], bf16)
        s2_cur = sb("s2_cur", [P, NODES])
        s2_masked = sb("s2_masked", [P, NODES])
        row_max = sb("row_max", [P, 1])
        s1_cur = sb("s1_cur", [P, 1])
        e = sb("e", [P, NODES])
        e_max = sb("e_max", [P, 1])
        neg_max = sb("neg_max", [P, 1])
        prob_t = sb("prob_t", [P, CHUNKS, 4, P])
        inv_sum = sb("inv_sum", [P, 1])
        x1_att = sb("x1_att", [P, 2, CH])
        result = sb("result", [P, 2, CH])

        ha_ps = ps("ha_ps", [P, 4, P])
        y_ps = ps("y_ps", [P, 512])
        h2_ps = ps("h2_ps", [P, 4, P])
        wh_ps = ps("wh_ps", [P, 512])
        s2_ps = ps("s2_ps", [P, 512])
        pt_ps = [ps(f"pt_ps{i}", [P, 4, P]) for i in range(2)]
        att_ps = ps("att_ps", [P, 512])

        weights_loaded = sem("weights_loaded")
        pool_consts_made = sem("pool_consts_made")
        dve_consts_made = sem("dve_consts_made")
        wa_made = sem("wa_made")
        zeros_made, zero_stored = sem("zeros_made"), sem("zero_stored")
        x_norm_loaded, adj_pick_loaded, x_upd_loaded = sem2("x_norm_loaded"), sem("adj_pick_loaded"), sem2("x_upd_loaded")
        h_upd_loaded, adj_att_loaded, x1_att_loaded = sem2("h_upd_loaded"), sem("adj_att_loaded"), sem2("x1_att_loaded")
        rows_loaded = sem2("rows_loaded")
        h_stored, x1_stored, result_stored = sem2("h_stored"), sem2("x1_stored"), sem2("result_stored")
        ln_step_made, ln_shift_made, h_made = sem("ln_step_made"), sem("ln_shift_made"), sem("h_made")
        keys_made, top_made, picks_made = sem("keys_made"), sem("top_made"), sem("picks_made")
        agg_made, ha_ps_made, ha_t_made, y_made = sem("agg_made"), sem("ha_ps_made"), sem("ha_t_made"), sem("y_made")
        x1_made, h2_made = sem("x1_made"), sem("h2_made")
        h2_ps_made, h2_t_made, wh_ps_made = sem("h2_ps_made"), sem("h2_t_made"), sem("wh_ps_made")
        s2_ps_made, s2_made = sem("s2_ps_made"), sem("s2_made")
        s2_cur_made, mask_made, masked_made = sem("s2_cur_made"), sem("mask_made"), sem("masked_made")
        pre_made, e_made, top_pre_made = sem("pre_made"), sem("e_made"), sem("top_pre_made")
        neg_max_made, prob_made = sem("neg_max_made"), sem("prob_made")
        pt_ps_made, pt_made, att_made = sem("pt_ps_made"), sem("pt_made"), sem("att_made")
        inv_made, result_made = sem("inv_made"), sem("result_made")

        block = ctx.enter_context(nc.Block())

        def in_slot(tile, slot):
            return (tile - slot) // 2 + 1

        @block.sync
        def _(sp):
            sp.wait_ge(zeros_made, 1)
            sp.dma_start(table[NODES:TABLE_ROWS, :], rows[0:1, 0, 0:CH]).then_inc(zero_stored, 16)
            others = table[TABLE_ROWS:TABLE_GRAPHS * TABLE_ROWS, :].rearrange("r c -> (r c)")
            sp.dma_start(others.rearrange("(p f) -> p f", p=P),
                         rows[:].rearrange("p s f -> p (s f)")[:, 0:ZERO_RUN]).then_inc(zero_stored, 16)
            sp.dma_start(w0_sb[:], w0.rearrange("(k p) o -> p k o", p=P)).then_inc(weights_loaded, 16)
            sp.dma_start(b0_sb[:], b0.rearrange("(a n) -> a n", a=1)).then_inc(weights_loaded, 16)
            sp.dma_start(w1s[:, :, 0:CH], w1.rearrange("(k p) o -> p k o", p=P)).then_inc(weights_loaded, 16)
            sp.dma_start(a_bc[:], a1.rearrange("n a -> a n").broadcast_to([P, 2 * CH])).then_inc(weights_loaded, 16)

            def step(base, slot, stages):
                k = base + slot
                nrm, upd, att = k + NORM_LEAD, k - UPDATE_LAG, k - ATTEND_LAG
                if "a" in stages:
                    wait(sp, mask_made, att)
                    sp.dma_start(adj_att[:], tile_rows(adj_rows, att)).then_inc(adj_att_loaded, 16)
                if "n" in stages:
                    wait(sp, h_made, nrm - 1)
                    sp.dma_start(x_norm[:, slot, :], tile_rows(x_rows, nrm)).then_inc(x_norm_loaded[slot], 16)
                if "p" in stages:
                    wait(sp, keys_made, k)
                    sp.dma_start(adj_pick[:], tile_rows(adj_rows, k)).then_inc(adj_pick_loaded, 16)
                if "u" in stages:
                    wait(sp, x1_made, upd - 1)
                    sp.dma_start(x_upd[:, slot, :], tile_rows(x_rows, upd)).then_inc(x_upd_loaded[slot], 16)
                    wait(sp, ha_ps_made, upd - 1)
                    wait(sp, h_stored[slot], in_slot(upd, slot) * 16)
                    sp.dma_start(h_upd[:, slot, :], table_tile(upd)).then_inc(h_upd_loaded[slot], 16)
                if "a" in stages:
                    wait(sp, result_made, att - 1)
                    wait(sp, x1_stored[slot], in_slot(att, slot) * 16)
                    sp.dma_start(x1_att[:, slot, :], tile_rows(x1_rows, att)).then_inc(x1_att_loaded[slot], 16)

            run_steps(sp, step)
            for stored in (*h_stored, *x1_stored, *result_stored):
                sp.wait_ge(stored, TILES // 2 * 16)
            sp.wait_ge(zero_stored, 32)

        @block.gpsimd
        def _(pool):
            pool.memset(ident_zero[:], 0.0).then_inc(pool_consts_made, 1)
            pool.memset(ones[:], 1.0).then_inc(pool_consts_made, 1)
            pool.iota(s2_masked[:].bitcast(i32), [[-1, NODES]], base=NODES,
                      channel_multiplier=0).then_inc(pool_consts_made, 1)
            pool.iota(table_base_i[:], [[0, 3], [TABLE_ROWS, TABLE_GRAPHS]], base=NODES,
                      channel_multiplier=0).then_inc(pool_consts_made, 1)
            pool.wait_ge(pool_consts_made, 4)
            pool.affine_select(out=ident[:], in_=ident_zero[:], compare_op=ALU.not_equal, fill=1.0, base=0,
                               pattern=[[-1, P]], channel_multiplier=1).then_inc(pool_consts_made, 1)
            pool.wait_ge(zero_stored, 32)

            def step(base, slot, stages):
                k = base + slot
                if "p" in stages:
                    graph = k // TILES_PER_GRAPH
                    for stored in h_stored:
                        pool.wait_ge(stored, (graph + 1) * (TILES_PER_GRAPH // 2 * 16))
                    wait(pool, agg_made, k - 1)
                    hold(pool, picks_made, k + 1)
                    for i in range(PICKS):
                        pool.indirect_dma_start(
                            out=rows[:, slot, i * CH:(i + 1) * CH], out_offset=None, in_=table,
                            in_offset=bass.IndirectOffsetOnAxis(ap=picks[:, slot, i:i + 1], axis=0),
                        ).then_inc(rows_loaded[slot], 16)

            run_steps(pool, step)

        @block.vector
        def _(dve):
            dve.memset(rows[:].rearrange("p s f -> p (s f)")[:, 0:ZERO_RUN], 0.0).then_inc(zeros_made, 1)
            dve.wait_ge(pool_consts_made, 5)
            dve.tensor_copy(countdown[:], s2_masked[:].bitcast(i32)).then_inc(dve_consts_made, 1)
            dve.tensor_copy(table_base[:], table_base_i[:]).then_inc(dve_consts_made, 1)
            dve.memset(wh[:, :, CH:CH + 1], 1.0).then_inc(dve_consts_made, 1)
            dve.wait_ge(weights_loaded, 64)
            for half in range(2):
                for k in range(2):
                    n = 2 * half + k
                    dve.tensor_tensor(a_prod[:], w1s[:, k, 0:CH], a_bc[:, half * CH:(half + 1) * CH],
                                      ALU.mult).then_inc(wa_made, 1)
                    dve.wait_ge(wa_made, 2 * n + 1)
                    dve.tensor_reduce(out=wa[:, n:n + 1], in_=a_prod[:], axis=AX.X, op=ALU.add).then_inc(wa_made, 1)
                    dve.wait_ge(wa_made, 2 * n + 2)
            for k in range(2):
                dve.tensor_copy(w1s[:, k, CH:CH + 1], wa[:, k:k + 1]).then_inc(dve_consts_made, 1)
                dve.tensor_scalar(w2_bc[:, k, :], ones[:], wa[:, 2 + k:3 + k], None,
                                  ALU.mult).then_inc(dve_consts_made, 1)
            dve.wait_ge(dve_consts_made, 7)

            def step(base, slot, stages):
                k = base + slot
                nrm, upd, att = k + NORM_LEAD, k - UPDATE_LAG, k - ATTEND_LAG
                if "a" in stages:
                    dve.wait_ge(adj_att_loaded, (att + 1) * 16)
                    dve.tensor_scalar(off_mask[:], adj_att[:], 0, NEG_BIG, ALU.is_le,
                                      ALU.mult).then_inc(mask_made, 1)
                if "a" in stages:
                    dve.wait_ge(mask_made, att + 1)
                    dve.wait_ge(s2_cur_made, att + 1)
                    wait(dve, pre_made, att)
                    dve.nop(nofuse=True)
                    dve.tensor_tensor_reduce(out=s2_masked[:], in0=s2_cur[:], in1=off_mask[:], scale=1.0,
                                             scalar=-3.0e38, op0=ALU.add, op1=ALU.max,
                                             accum_out=row_max[:]).then_inc(masked_made, 1)
                if "u" in stages:
                    dve.wait_ge(rows_loaded[slot], in_slot(upd, slot) * (PICKS * 16))
                    wait(dve, ha_ps_made, upd)
                    dve.tensor_reduce(out=agg[:], in_=rows[:, slot, :].rearrange("p (k c) -> p c k", c=CH),
                                      axis=AX.X, op=ALU.max).then_inc(agg_made, 1)
                if "a" in stages:
                    dve.wait_ge(masked_made, att + 1)
                    dve.wait_ge(pre_made, att + 1)
                    dve.tensor_scalar(e_max[:], row_max[:], s1_cur[:], -1.0, ALU.add,
                                      ALU.mult).then_inc(top_pre_made, 1)
                    dve.scalar_tensor_tensor(e[:], e[:], LEAKY_SLOPE, e[:], ALU.mult, ALU.max).then_inc(e_made, 1)
                    dve.wait_ge(top_pre_made, att + 1)
                    wait(dve, prob_made, att)
                    dve.scalar_tensor_tensor(neg_max[:], e_max[:], LEAKY_SLOPE, e_max[:], ALU.mult,
                                             ALU.min).then_inc(neg_max_made, 1)

                def next_eight(n):
                    dve.max(top[:, 8 * n:8 * n + 8], keys[:, n % 2, :]).then_inc(top_made, 1)
                    hold(dve, top_made, k * (2 * ROUNDS - 1) + 2 * n + 1)

                def drop_eight(n):
                    dve.match_replace(keys[:, 1 - n % 2, :], top[:, 8 * n:8 * n + 8], keys[:, n % 2, :],
                                      0.0).then_inc(top_made, 1)
                    hold(dve, top_made, k * (2 * ROUNDS - 1) + 2 * n + 2)

                if "p" in stages:
                    dve.wait_ge(adj_pick_loaded, (k + 1) * 16)
                    dve.scalar_tensor_tensor(keys[:, 0, :], adj_pick[:], 0, countdown[:], ALU.not_equal,
                                             ALU.mult).then_inc(keys_made, 1)
                    hold(dve, keys_made, k + 1)
                    next_eight(0)
                    drop_eight(0)
                    next_eight(1)
                    drop_eight(1)
                if "u" in stages:
                    dve.wait_ge(y_made, upd + 1)
                    dve.wait_ge(x_upd_loaded[slot], in_slot(upd, slot) * 16)
                    wait(dve, x1_stored[slot], (in_slot(upd, slot) - 1) * 16)
                    dve.scalar_tensor_tensor(x1[:, slot, :], y_ps[:, 0:CH], 0.0, x_upd[:, slot, :], ALU.max,
                                             ALU.add).then_inc(x1_made, 1)
                if "n" in stages or "u" in stages:
                    norm_steps = k + NORM_LEAD
                    ops = [0]

                    def made(instruction):
                        instruction.then_inc(ln_step_made, 1)
                        ops[0] += 1
                        hold(dve, ln_step_made, norm_steps * LN_OPS + ops[0])

                    if "n" in stages:
                        dve.wait_ge(x_norm_loaded[slot], in_slot(nrm, slot) * 16)
                        last = dve.bn_stats(ln_stats[:, 0, :], x_norm[:, slot, :])
                    if "u" in stages:
                        dve.wait_ge(x1_made, upd + 1)
                        last = dve.bn_stats(ln_stats[:, 1, :], x1[:, slot, :])
                    c = slice(0 if "n" in stages else 1, 2 if "u" in stages else 1)
                    made(last)
                    if "n" in stages:
                        last = dve.bn_aggr(ln_mv[:, 0, :], ln_stats[:, 0, :])
                    if "u" in stages:
                        last = dve.bn_aggr(ln_mv[:, 1, :], ln_stats[:, 1, :])
                    made(last)
                    made(dve.tensor_scalar(ln_var[:, c], ln_mv[:, c, 1], LN_EPS, None, ALU.add))
                    made(dve.tensor_scalar(ln_root[:, c].bitcast(i32), ln_var[:, c].bitcast(i32), -0.5,
                                           float(ROOT_GUESS), ALU.mult, ALU.add))
                    if "n" in stages:
                        wait(dve, h_made, nrm - 1)
                    if "u" in stages:
                        wait(dve, h2_made, upd - 1)
                    for i in range(NEWTON_STEPS):
                        made(dve.tensor_tensor(ln_err[:, c], ln_root[:, c], ln_root[:, c], ALU.mult))
                        made(dve.scalar_tensor_tensor(ln_err[:, c], ln_err[:, c], -0.5, ln_var[:, c], ALU.mult, ALU.mult))
                        to = ln_scale[:, slot, c] if i == NEWTON_STEPS - 1 else ln_root[:, c]
                        made(dve.scalar_tensor_tensor(to, ln_err[:, c], 1.5, ln_root[:, c], ALU.add, ALU.mult))
                    dve.scalar_tensor_tensor(ln_shift[:, slot, c], ln_mv[:, c, 0], -1.0, ln_scale[:, slot, c],
                                             ALU.mult, ALU.mult).then_inc(ln_shift_made, 1)
                if "p" in stages:
                    next_eight(2)
                    drop_eight(2)
                    next_eight(3)
                    dve.tensor_scalar(picks[:, slot, :], top[:, 0:PICKS], -1.0,
                                      table_base[:, bass.ds(k // TILES_PER_GRAPH, 1)], ALU.mult,
                                      ALU.add).then_inc(picks_made, 1)
                if "a" in stages:
                    dve.wait_ge(att_made, att + 1)
                    dve.reciprocal(inv_sum[:], att_ps[:, CH:CH + 1]).then_inc(inv_made, 1)
                    dve.wait_ge(inv_made, att + 1)
                    dve.wait_ge(x1_att_loaded[slot], in_slot(att, slot) * 16)
                    wait(dve, result_stored[slot], (in_slot(att, slot) - 1) * 16)
                    dve.scalar_tensor_tensor(result[:, slot, :], att_ps[:, 0:CH], inv_sum[:], x1_att[:, slot, :],
                                             ALU.mult, ALU.add).then_inc(result_made, 1)

            run_steps(dve, step)

        @block.scalar
        def _(act):
            def step(base, slot, stages):
                k = base + slot
                nrm, upd, att = k + NORM_LEAD, k - UPDATE_LAG, k - ATTEND_LAG
                if "a" in stages:
                    graph = att // TILES_PER_GRAPH
                    act.wait_ge(s2_made, (graph + 1) * TILES_PER_GRAPH)
                    wait(act, neg_max_made, att)
                    act.activation(s1_cur[:], s1[:, bass.ds(att % (2 * TILES_PER_GRAPH), 1)], ACT.Copy)
                    wait(act, masked_made, att)
                    act.activation(s2_cur[:], s2[:, bass.ds(graph % 2 * NODES, NODES)],
                                   ACT.Copy).then_inc(s2_cur_made, 1)
                    act.wait_ge(s2_cur_made, att + 1)
                    act.wait_ge(masked_made, att + 1)
                    wait(act, pt_ps_made, att * CHUNKS)
                    act.activation(e[:], s2_masked[:], ACT.Identity, bias=s1_cur[:]).then_inc(pre_made, 1)
                if "u" in stages:
                    act.wait_ge(ha_ps_made, upd + 1)
                    wait(act, y_made, upd)
                    act.activation(ha_t[:], ha_ps[:], ACT.Copy).then_inc(ha_t_made, 1)
                if "a" in stages:
                    act.wait_ge(neg_max_made, att + 1)
                    act.activation(e[:], e[:], ACT.Exp, bias=neg_max[:]).then_inc(prob_made, 1)
                    for q in range(CHUNKS):
                        act.wait_ge(pt_ps_made, att * CHUNKS + q + 1)
                        if q == 0:
                            wait(act, att_made, att)
                        act.activation(prob_t[:, q, :, :], pt_ps[q % 2][:], ACT.Copy).then_inc(pt_made, 1)
                if "u" in stages:
                    act.wait_ge(ln_shift_made, nrm + 1)
                    wait(act, h2_ps_made, upd)
                    act.activation(h2[:], x1[:, slot, :], ACT.Relu, bias=ln_shift[:, slot, 1:2],
                                   scale=ln_scale[:, slot, 1:2]).then_inc(h2_made, 1)
                    act.dma_start(tile_rows(x1_rows, upd), x1[:, slot, :]).then_inc(x1_stored[slot], 16)
                    act.wait_ge(h2_ps_made, upd + 1)
                    wait(act, s2_ps_made, upd)
                    act.activation(h2_t[:], h2_ps[:, 0:2, :], ACT.Copy).then_inc(h2_t_made, 1)
                    place = upd % (2 * TILES_PER_GRAPH)
                    act.wait_ge(wh_ps_made, upd + 1)
                    act.activation(wh[:, bass.ds(place, 1), 0:CH], wh_ps[:, 0:CH], ACT.Copy)
                    act.activation(s1[:, bass.ds(place, 1)], wh_ps[:, CH:CH + 1], ACT.Copy)
                    act.wait_ge(s2_ps_made, upd + 1)
                    act.activation(s2[:, bass.ds(place * P, P)], s2_ps[:, 0:P], ACT.Copy).then_inc(s2_made, 1)
                if "n" in stages:
                    act.wait_ge(ln_shift_made, nrm + 1)
                    wait(act, h_stored[slot], (in_slot(nrm, slot) - 1) * 16)
                    act.activation(h_out[:, slot, :], x_norm[:, slot, :], ACT.Relu, bias=ln_shift[:, slot, 0:1],
                                   scale=ln_scale[:, slot, 0:1]).then_inc(h_made, 1)
                    if isinstance(k, int) and nrm == TILES_PER_GRAPH:
                        act.wait_ge(zero_stored, 32)
                    act.wait_ge(h_made, nrm + 1)
                    act.dma_start(table_tile(nrm), h_out[:, slot, :]).then_inc(h_stored[slot], 16)
                if "a" in stages:
                    act.wait_ge(result_made, att + 1)
                    act.dma_start(tile_rows(out_rows, att), result[:, slot, :]).then_inc(result_stored[slot], 16)

            run_steps(act, step)

        @block.tensor
        def _(pe):
            pe.wait_ge(pool_consts_made, 5)
            pe.wait_ge(weights_loaded, 64)
            pe.wait_ge(dve_consts_made, 7)

            def step(base, slot, stages):
                k = base + slot
                upd, att = k - UPDATE_LAG, k - ATTEND_LAG
                if "u" in stages:
                    pe.wait_ge(h_upd_loaded[slot], in_slot(upd, slot) * 16)
                    pe.wait_ge(agg_made, upd + 1)
                    wait(pe, ha_t_made, upd)
                    for j in range(4):
                        half = (h_upd[:, slot, :] if j < 2 else agg[:])[:, j % 2 * P:(j % 2 + 1) * P]
                        last = pe.transpose(ha_ps[:, j, :], half, ident[:])
                    last.then_inc(ha_ps_made, 1)
                    pe.wait_ge(ha_t_made, upd + 1)
                    wait(pe, x1_made, upd)
                    for j in range(4):
                        pe.matmul(y_ps[:, 0:CH], ha_t[:, j, :], w0_sb[:, j, :], start=j == 0, stop=False)
                    pe.matmul(y_ps[:, 0:CH], ones[0:1, :], b0_sb[:], start=False, stop=True).then_inc(y_made, 1)

                def transpose_chunk(q):
                    chunk = att * CHUNKS + q
                    wait(pe, pt_made, chunk - 1)
                    for j in range(4):
                        col = (4 * q + j) * P
                        last = pe.transpose(pt_ps[q % 2][:, j, :], e[:, col:col + P], ident[:])
                    last.then_inc(pt_ps_made, 1)

                def multiply_chunk(q):
                    pe.wait_ge(pt_made, att * CHUNKS + q + 1)
                    for j in range(4):
                        node_tile = 4 * q + j
                        last = pe.matmul(att_ps[:, 0:CH + 1], prob_t[:, q, j, :],
                                         wh[:, bass.ds(att // TILES_PER_GRAPH % 2 * TILES_PER_GRAPH + node_tile, 1), :],
                                         start=node_tile == 0, stop=node_tile == TILES_PER_GRAPH - 1)
                    if q == CHUNKS - 1:
                        last.then_inc(att_made, 1)

                if "a" in stages:
                    pe.wait_ge(prob_made, att + 1)
                    transpose_chunk(0)
                    wait(pe, result_made, att)
                    pe.wait_ge(s2_made, (att // TILES_PER_GRAPH + 1) * TILES_PER_GRAPH)
                    for q in range(1, CHUNKS):
                        transpose_chunk(q)
                        multiply_chunk(q - 1)
                    multiply_chunk(CHUNKS - 1)
                if "u" in stages:
                    pe.wait_ge(h2_made, upd + 1)
                    wait(pe, h2_t_made, upd)
                    for j in range(2):
                        last = pe.transpose(h2_ps[:, j, :], h2[:, j * P:(j + 1) * P], ident[:])
                    last.then_inc(h2_ps_made, 1)
                    pe.wait_ge(h2_t_made, upd + 1)
                    wait(pe, s2_made, upd)
                    for j in range(2):
                        last = pe.matmul(wh_ps[:, 0:CH + 1], h2_t[:, j, :], w1s[:, j, :], start=j == 0, stop=j == 1)
                    last.then_inc(wh_ps_made, 1)
                    for j in range(2):
                        last = pe.matmul(s2_ps[:, 0:P], w2_bc[:, j, :], h2_t[:, j, :], start=j == 0, stop=j == 1)
                    last.then_inc(s2_ps_made, 1)

            run_steps(pe, step)


_INS = ["x", "adj", "L0_gnn_W", "L0_gnn_b", "L1_gnn_W", "L1_gnn_a"]


def kernel(**inputs):
    import numpy as np
    import concourse.bacc as bacc
    from concourse.bass_utils import run_bass_kernel_spmd

    nc = bacc.Bacc("TRN2", target_bir_lowering=False, num_devices=1)
    arrays, args = {}, []
    for name in _INS:
        array = np.ascontiguousarray(inputs[name])
        arrays[name] = array
        args.append(nc.dram_tensor(name, array.shape, mybir.dt.from_np(array.dtype), kind="ExternalInput").ap())
    out = nc.dram_tensor("out", (GRAPHS, NODES, CH), mybir.dt.float32, kind="ExternalOutput").ap()
    graph_layers(nc, *args, out)
    ran = run_bass_kernel_spmd(nc, [arrays], core_ids=[0])
    return ran.results[0]["out"]
```

```python
from contextlib import ExitStack

import concourse.bass as bass
from concourse import mybir

P = 128
GRAPHS, NODES, CH = 8, 2048, 256
PICKS = 25
TILES_PER_GRAPH = NODES // P
TILES = GRAPHS * TILES_PER_GRAPH
TABLE_ROWS = NODES + 1
TABLE_GRAPHS = 3
ZERO_RUN = (TABLE_GRAPHS - 1) * TABLE_ROWS * CH // P
ROUNDS = (PICKS + 7) // 8
GROUP = 8
GROUPS = NODES // GROUP
TOP = 8 * ROUNDS
NORM_LEAD, UPDATE_LAG, ATTEND_LAG, RESULT_LAG = 18, 2, 18, 19
LN_EPS = 1e-5
NEWTON_STEPS = 3
ROOT_GUESS = 0x5F3759DF
LEAKY_SLOPE = 0.2
NEG_BIG = -9e15
CHUNKS = NODES // 512

PHASES = [
    (0, 2, "np", "np"),
    (2, 4, "npu", "npu"),
    (4, 18, "npu", "npu"),
    (18, 20, "npua", "npuar"),
    (20, 110, "npuar", "npuar"),
    (110, 128, "puar", "puar"),
    (128, 130, "uar", "uar"),
    (130, 146, "ar", "ar"),
    (146, 148, "r", ""),
]


def run_steps(eng, body):
    for first, end, even, odd in PHASES:
        if end - first == 2:
            body(first, 0, even)
            body(first + 1, 1, odd)
            continue
        with eng.Fori(0, (end - first) // 2) as pair:
            body(pair * 2 + first, 0, even)
            body(pair * 2 + (first + 1), 1, odd)


def wait(eng, sem, count):
    if not isinstance(count, int) or count > 0:
        eng.wait_ge(sem, count)


def hold(eng, sem, count):
    eng.wait_ge(sem, count)
    eng.nop(nofuse=True)


def in_slot(tile, slot):
    return (tile - slot) // 2 + 1


def graph_layers(nc, x, adj, w0, b0, w1, a1, out):
    fp32, bf16 = mybir.dt.float32, mybir.dt.bfloat16
    i32, u32 = mybir.dt.int32, mybir.dt.uint32
    ALU = mybir.AluOpType
    ACT = mybir.ActivationFunctionType
    AX = mybir.AxisListType

    x_rows = x.rearrange("g n c -> (g n) c")
    adj_rows = adj.rearrange("g n m -> (g n) m")
    out_rows = out.rearrange("g n c -> (g n) c")
    table = nc.dram_tensor("table", [TABLE_GRAPHS * TABLE_ROWS, CH], fp32, kind="Internal").ap()
    x1_rows = nc.dram_tensor("x1_rows", [GRAPHS * NODES, CH], fp32, kind="Internal").ap()

    def tile_rows(rows, tile):
        return rows[bass.ds(tile * P, P), :]

    def table_tile(tile):
        graph_slot = tile // TILES_PER_GRAPH % TABLE_GRAPHS
        return table[bass.ds(graph_slot * TABLE_ROWS + tile % TILES_PER_GRAPH * P, P), :]

    with ExitStack() as ctx:
        def sb(name, shape, dt=fp32):
            return ctx.enter_context(nc.sbuf_tensor(name, shape, dt))

        def ps(name, shape, dt=fp32):
            return ctx.enter_context(nc.psum_tensor(name, shape, dt))

        def sem(name):
            return ctx.enter_context(nc.semaphore(name))

        def sem2(name):
            return [sem(f"{name}{i}") for i in range(2)]

        ident = sb("ident", [P, P])
        ident_b = sb("ident_b", [P, P], bf16)
        ones = sb("ones", [P, P])
        byte_w = sb("byte_w", [P, P // GROUP], bf16)
        group_base = sb("group_base", [P, GROUPS])
        group_bits = sb("group_bits", [P, TOP, GROUP], i32)
        group_off = sb("group_off", [P, TOP, GROUP], i32)
        table_base = sb("table_base", [P, 9])
        w0_sb = sb("w0_sb", [P, 4, CH])
        b0_sb = sb("b0_sb", [1, CH])
        w1s = sb("w1s", [P, 2, CH + 1])
        wa = sb("wa", [P, 4])
        w2_bc = sb("w2_bc", [P, 2, P])
        ln_stats = sb("ln_stats", [P, NORM_LEAD, 6])
        ln_mv = sb("ln_mv", [P, NORM_LEAD, 2])
        ln_var = sb("ln_var", [P, NORM_LEAD])
        ln_root = sb("ln_root", [P, NORM_LEAD])
        ln_err = sb("ln_err", [P, NORM_LEAD])
        ln_scale = sb("ln_scale", [P, 2, 2])
        ln_shift = sb("ln_shift", [P, 2, 2])
        first_scale = sb("first_scale", [P, NORM_LEAD])
        first_shift = sb("first_shift", [P, NORM_LEAD])
        x_norm = sb("x_norm", [P, 2, CH])
        h_out = sb("h_out", [P, 2, CH])
        adj_pick = sb("adj_pick", [P, NODES], i32)
        is_nbr = sb("is_nbr", [P, NODES], bf16)
        is_nbr_t = sb("is_nbr_t", [P, TILES_PER_GRAPH, P], bf16)
        group_val = sb("group_val", [P, 2, GROUPS])
        top_val = sb("top_val", [P, TOP])
        top_int = sb("top_int", [P, TOP], i32)
        top_col = sb("top_col", [P, TOP], i32)
        nbr_bits = sb("nbr_bits", [P, TOP, GROUP], i32)
        col_keys = sb("col_keys", [P, TOP, GROUP])
        keys = sb("keys", [P, 2, TOP * GROUP])
        top_keys = sb("top_keys", [P, TOP])
        picks = sb("picks", [P, 2, PICKS], u32)
        rows = sb("rows", [P, 2, PICKS * CH])
        x_upd = sb("x_upd", [P, 2, CH])
        h_upd = sb("h_upd", [P, 2, CH])
        agg = sb("agg", [P, CH])
        ha_t = sb("ha_t", [P, 4, P])
        x1 = sb("x1", [P, 2, CH])
        h2 = sb("h2", [P, CH])
        h2_t = sb("h2_t", [P, 2, P])
        wh = sb("wh", [P, 2 * TILES_PER_GRAPH, CH + 1])
        s1 = sb("s1", [P, 2 * TILES_PER_GRAPH])
        s2 = sb("s2", [P, 2 * NODES])
        adj_att = sb("adj_att", [P, NODES], i32)
        off_mask = sb("off_mask", [P, NODES], bf16)
        s2_cur = sb("s2_cur", [P, NODES])
        row_max = sb("row_max", [P, 1])
        s1_cur = sb("s1_cur", [P, 2])
        e = sb("e", [P, 2, NODES])
        neg_pre = sb("neg_pre", [P, 1])
        neg_max = sb("neg_max", [P, 2])
        prob_t = sb("prob_t", [P, CHUNKS, 4, P])
        inv_sum = sb("inv_sum", [P, 1])
        x1_att = sb("x1_att", [P, 2, CH])
        result = sb("result", [P, 2, CH])

        zeros = wh[:].rearrange("p t c -> p (t c)")[:, 0:ZERO_RUN]
        first_x = rows[:, 0, 0:NORM_LEAD * CH].rearrange("p (t c) -> p t c", c=CH)
        first_h = rows[:, 1, 0:NORM_LEAD * CH].rearrange("p (t c) -> p t c", c=CH)
        a_bc, a_prod = e[:, 0, 0:2 * CH], e[:, 0, 2 * CH:3 * CH]
        ident_zero = e[:, 1, 0:P]
        group_base_i = adj_pick[:, 0:GROUPS]
        table_base_i = adj_pick[:, GROUPS:GROUPS + 9]

        update_ps = ps("update_ps", [P, 512])
        y_ps, wh_ps, s2_ps = update_ps[:, 0:CH], update_ps[:, 0:CH + 1], update_ps[:, CH + 128:CH + 256]
        nbr_ps = [ps(f"nbr_ps{i}", [P, 8, P], bf16) for i in range(2)]
        byte_ps = ps("byte_ps", [P, 512])
        pt_ps = [ps(f"pt_ps{i}", [P, 4, P]) for i in range(2)]
        att_ps = ps("att_ps", [P, 512])

        weights_loaded, x_first_loaded = sem("weights_loaded"), [sem(f"x_first_loaded{i}") for i in range(3)]
        pool_made, dve_consts_made, wa_made = sem("pool_made"), sem("dve_consts_made"), sem("wa_made")
        ident_made, first_shift_made = sem("ident_made"), sem("first_shift_made")
        zeros_made, zero_stored = sem("zeros_made"), sem("zero_stored")
        x_norm_loaded, adj_pick_loaded, x_upd_loaded = sem2("x_norm_loaded"), sem("adj_pick_loaded"), sem2("x_upd_loaded")
        h_upd_loaded, adj_att_loaded, x1_att_loaded = sem2("h_upd_loaded"), sem("adj_att_loaded"), sem2("x1_att_loaded")
        rows_loaded = sem2("rows_loaded")
        h_stored, x1_stored, result_stored = sem2("h_stored"), sem2("x1_stored"), sem2("result_stored")
        dve_done = sem("dve_done")
        ln_shift_made, h_made = sem("ln_shift_made"), sem("h_made")
        nbr_made, nbr_ps_made, nbr_t_made, byte_made = sem("nbr_made"), sem("nbr_ps_made"), sem("nbr_t_made"), sem("byte_made")
        vals_made, picks_made = sem("vals_made"), sem("picks_made")
        agg_made, ha_ps_made, ha_t_made, y_made = sem("agg_made"), sem("ha_ps_made"), sem("ha_t_made"), sem("y_made")
        x1_made, h2_made, h2_ps_made, h2_t_made = sem("x1_made"), sem("h2_made"), sem("h2_ps_made"), sem("h2_t_made")
        wh_ps_made, s2_made = sem("wh_ps_made"), sem("s2_made")
        s2_cur_made, mask_made, masked_made = sem("s2_cur_made"), sem("mask_made"), sem("masked_made")
        pre_made, neg_max_made, prob_made = sem("pre_made"), sem("neg_max_made"), sem("prob_made")
        pt_ps_made, pt_made, att_made = sem("pt_ps_made"), sem("pt_made"), sem("att_made")
        result_made = sem("result_made")

        block = ctx.enter_context(nc.Block())

        @block.sync
        def _(sp):
            third = NORM_LEAD // 3
            for i, loaded in enumerate(x_first_loaded):
                sp.dma_start(first_x[:, i * third:(i + 1) * third, :],
                             x_rows[i * third * P:(i + 1) * third * P, :].rearrange("(t p) c -> p t c", p=P)
                             ).then_inc(loaded, 16)
            sp.dma_start(w1s[:, :, 0:CH], w1.rearrange("(k p) o -> p k o", p=P)).then_inc(weights_loaded, 16)
            sp.dma_start(a_bc, a1.rearrange("n a -> a n").broadcast_to([P, 2 * CH])).then_inc(weights_loaded, 16)
            sp.dma_start(w0_sb[:], w0.rearrange("(k p) o -> p k o", p=P)).then_inc(weights_loaded, 16)
            sp.dma_start(b0_sb[:], b0.rearrange("(a n) -> a n", a=1)).then_inc(weights_loaded, 16)
            sp.wait_ge(zeros_made, 1)
            sp.dma_start(table[NODES:TABLE_ROWS, :], zeros[0:1, 0:CH]).then_inc(zero_stored, 16)
            others = table[TABLE_ROWS:TABLE_GRAPHS * TABLE_ROWS, :].rearrange("r c -> (r c)")
            sp.dma_start(others.rearrange("(p f) -> p f", p=P), zeros).then_inc(zero_stored, 16)

            def step(k, slot, stages):
                nrm, upd, att = k + NORM_LEAD, k - UPDATE_LAG, k - ATTEND_LAG
                if "p" in stages:
                    if isinstance(k, int) and k == 0:
                        sp.wait_ge(dve_consts_made, 2)
                    wait(sp, nbr_made, k)
                    sp.dma_start(adj_pick[:], tile_rows(adj_rows, k)).then_inc(adj_pick_loaded, 16)
                if "a" in stages:
                    wait(sp, mask_made, att)
                    sp.dma_start(adj_att[:], tile_rows(adj_rows, att)).then_inc(adj_att_loaded, 16)
                if "u" in stages:
                    wait(sp, x1_made, upd - 1)
                    sp.dma_start(x_upd[:, slot, :], tile_rows(x_rows, upd)).then_inc(x_upd_loaded[slot], 16)
                    wait(sp, ha_ps_made, upd - 1)
                    wait(sp, h_stored[slot], in_slot(upd, slot) * 16)
                    sp.dma_start(h_upd[:, slot, :], table_tile(upd)).then_inc(h_upd_loaded[slot], 16)
                if "a" in stages:
                    wait(sp, result_made, att - 1)
                    wait(sp, x1_stored[slot], in_slot(att, slot) * 16)
                    sp.dma_start(x1_att[:, slot, :], tile_rows(x1_rows, att)).then_inc(x1_att_loaded[slot], 16)
                if "n" in stages:
                    wait(sp, h_made, nrm - 1)
                    sp.dma_start(x_norm[:, slot, :], tile_rows(x_rows, nrm)).then_inc(x_norm_loaded[slot], 16)

            run_steps(sp, step)
            for stored in (*h_stored, *x1_stored, *result_stored):
                sp.wait_ge(stored, TILES // 2 * 16)
            sp.wait_ge(zero_stored, 32)

        @block.gpsimd
        def _(pool):
            pool.memset(ident_zero, 0.0).then_inc(pool_made, 1)
            pool.memset(ones[:], 1.0).then_inc(pool_made, 1)
            pool.memset(byte_w[:], 0.0).then_inc(pool_made, 1)
            pool.iota(group_base_i, [[-GROUPS, GROUPS]], base=GROUPS * GROUPS, channel_multiplier=0).then_inc(pool_made, 1)
            pool.iota(table_base_i, [[0, 3], [TABLE_ROWS, TABLE_GRAPHS]], base=NODES,
                      channel_multiplier=0).then_inc(pool_made, 1)
            pool.iota(group_off[:], [[0, TOP], [1, GROUP]], base=0, channel_multiplier=0).then_inc(pool_made, 1)
            for o in range(GROUP):
                pool.memset(group_bits[:, :, o:o + 1], 1 << (GROUP - 1 - o)).then_inc(pool_made, 1)
            pool.wait_ge(pool_made, 14)
            pool.affine_select(out=ident[:], in_=ident_zero, compare_op=ALU.not_equal, fill=1.0, base=0,
                               pattern=[[-1, P]], channel_multiplier=1).then_inc(pool_made, 1)
            for o in range(GROUP):
                pool.affine_select(out=byte_w[:], in_=byte_w[:], compare_op=ALU.not_equal,
                                   fill=float(1 << (GROUP - 1 - o)), base=-o,
                                   pattern=[[-GROUP, P // GROUP]], channel_multiplier=1).then_inc(pool_made, 1)
                pool.wait_ge(pool_made, 16 + o)
            pool.wait_ge(zero_stored, 32)

            def step(k, slot, stages):
                if "p" in stages:
                    graph = k // TILES_PER_GRAPH
                    for stored in h_stored:
                        pool.wait_ge(stored, (graph + 1) * (TILES_PER_GRAPH // 2 * 16))
                    if isinstance(k, int) and k == 1:
                        for stored in h_stored:
                            pool.wait_ge(stored, NORM_LEAD // 2 * 16)
                    wait(pool, agg_made, k - 1)
                    hold(pool, picks_made, k + 1)
                    for i in range(PICKS):
                        pool.indirect_dma_start(
                            out=rows[:, slot, i * CH:(i + 1) * CH], out_offset=None, in_=table,
                            in_offset=bass.IndirectOffsetOnAxis(ap=picks[:, slot, i:i + 1], axis=0),
                        ).then_inc(rows_loaded[slot], 16)

            run_steps(pool, step)

        @block.vector
        def _(dve):
            done = [0]

            def own(instruction):
                instruction.then_inc(dve_done, 1)
                done[0] += 1
                dve.wait_ge(dve_done, done[0])

            def restart():
                dve.sem_clear(dve_done)
                done[0] = 0

            def largest(top, values):
                for n in range(ROUNDS):
                    eight = top[:, 8 * n:8 * n + 8]
                    own(dve.max(eight, values[:, n % 2, :]))
                    if n < ROUNDS - 1:
                        own(dve.match_replace(values[:, 1 - n % 2, :], eight, values[:, n % 2, :], 0.0))

            def norm_scale(scale, columns):
                var, root, err = ln_var[:, columns], ln_root[:, columns], ln_err[:, columns]
                own(dve.tensor_scalar(var, ln_mv[:, columns, 1], LN_EPS, None, ALU.add))
                own(dve.tensor_scalar(root.bitcast(i32), var.bitcast(i32), -0.5, float(ROOT_GUESS), ALU.mult, ALU.add))
                for i in range(NEWTON_STEPS):
                    own(dve.tensor_tensor(err, root, root, ALU.mult))
                    own(dve.scalar_tensor_tensor(err, err, -0.5, var, ALU.mult, ALU.mult))
                    own(dve.scalar_tensor_tensor(scale if i == NEWTON_STEPS - 1 else root, err, 1.5, root,
                                                 ALU.add, ALU.mult))

            dve.memset(zeros, 0.0).then_inc(zeros_made, 1)
            for tile in range(NORM_LEAD):
                if tile % (NORM_LEAD // 3) == 0:
                    dve.wait_ge(x_first_loaded[tile // (NORM_LEAD // 3)], 16)
                last = dve.bn_stats(ln_stats[:, tile, :], first_x[:, tile, :])
            own(last)
            for tile in range(NORM_LEAD):
                last = dve.bn_aggr(ln_mv[:, tile, :], ln_stats[:, tile, :])
            own(last)
            norm_scale(first_scale[:], slice(0, NORM_LEAD))
            dve.scalar_tensor_tensor(first_shift[:], ln_mv[:, :, 0], -1.0, first_scale[:], ALU.mult,
                                     ALU.mult).then_inc(first_shift_made, 1)
            dve.wait_ge(pool_made, 23)
            dve.tensor_copy(group_base[:], group_base_i).then_inc(dve_consts_made, 1)
            dve.tensor_copy(table_base[:], table_base_i).then_inc(dve_consts_made, 1)
            dve.tensor_copy(ident_b[:], ident[:]).then_inc(dve_consts_made, 1)
            dve.wait_ge(weights_loaded, 64)
            for half in range(2):
                for k in range(2):
                    n = 2 * half + k
                    own(dve.tensor_tensor(a_prod, w1s[:, k, 0:CH], a_bc[:, half * CH:(half + 1) * CH], ALU.mult))
                    own(dve.tensor_reduce(out=wa[:, n:n + 1], in_=a_prod, axis=AX.X, op=ALU.add))
            for k in range(2):
                dve.tensor_copy(w1s[:, k, CH:CH + 1], wa[:, k:k + 1]).then_inc(dve_consts_made, 1)
                dve.tensor_scalar(w2_bc[:, k, :], ones[:], wa[:, 2 + k:3 + k], None,
                                  ALU.mult).then_inc(dve_consts_made, 1)
            dve.wait_ge(zero_stored, 32)
            dve.memset(wh[:, :, CH:CH + 1], 1.0).then_inc(dve_consts_made, 1)
            dve.wait_ge(dve_consts_made, 8)

            def step(k, slot, stages):
                nrm, upd, att, res = k + NORM_LEAD, k - UPDATE_LAG, k - ATTEND_LAG, k - RESULT_LAG
                restart()
                if "p" in stages:
                    wait(dve, nbr_ps_made, k * 2)
                    dve.wait_ge(adj_pick_loaded, (k + 1) * 16)
                    dve.tensor_scalar(is_nbr[:], adj_pick[:], 0, None, ALU.not_equal).then_inc(nbr_made, 1)
                if "a" in stages:
                    dve.wait_ge(adj_att_loaded, (att + 1) * 16)
                    dve.tensor_scalar(off_mask[:], adj_att[:], 0, NEG_BIG, ALU.is_le,
                                      ALU.mult).then_inc(mask_made, 1)
                    dve.wait_ge(mask_made, att + 1)
                    wait(dve, pt_ps_made, (att - 1) * CHUNKS)
                    hold(dve, s2_cur_made, att + 1)
                    dve.tensor_tensor_reduce(out=e[:, slot, :], in0=s2_cur[:], in1=off_mask[:], scale=1.0,
                                             scalar=-3.0e38, op0=ALU.add, op1=ALU.max,
                                             accum_out=row_max[:]).then_inc(masked_made, 1)
                if "u" in stages:
                    dve.wait_ge(rows_loaded[slot], in_slot(upd, slot) * (PICKS * 16))
                    wait(dve, ha_ps_made, upd)
                    dve.tensor_reduce(out=agg[:], in_=rows[:, slot, :].rearrange("p (k c) -> p c k", c=CH),
                                      axis=AX.X, op=ALU.max).then_inc(agg_made, 1)
                if "r" in stages:
                    dve.wait_ge(att_made, res + 1)
                    own(dve.reciprocal(inv_sum[:], att_ps[:, CH:CH + 1]))
                    dve.wait_ge(x1_att_loaded[1 - slot], in_slot(res, 1 - slot) * 16)
                    wait(dve, result_stored[1 - slot], (in_slot(res, 1 - slot) - 1) * 16)
                    dve.scalar_tensor_tensor(result[:, 1 - slot, :], att_ps[:, 0:CH], inv_sum[:],
                                             x1_att[:, 1 - slot, :], ALU.mult, ALU.add).then_inc(result_made, 1)
                if "a" in stages:
                    dve.wait_ge(masked_made, att + 1)
                    dve.wait_ge(pre_made, att + 1)
                    own(dve.tensor_scalar(neg_pre[:], row_max[:], s1_cur[:, slot:slot + 1], -1.0, ALU.add, ALU.mult))
                    dve.scalar_tensor_tensor(e[:, slot, :], e[:, slot, :], LEAKY_SLOPE, e[:, slot, :], ALU.mult, ALU.max)
                    wait(dve, prob_made, att - 1)
                    dve.scalar_tensor_tensor(neg_max[:, slot:slot + 1], neg_pre[:], LEAKY_SLOPE, neg_pre[:], ALU.mult,
                                             ALU.min).then_inc(neg_max_made, 1)
                if "p" in stages:
                    dve.wait_ge(byte_made, k + 1)
                    own(dve.scalar_tensor_tensor(group_val[:, 1, :], byte_ps[:, 0:GROUPS], 0.0, group_base[:],
                                                 ALU.is_gt, ALU.mult))
                    dve.tensor_tensor(group_val[:, 0, :], group_val[:, 1, :], byte_ps[:, 0:GROUPS],
                                      ALU.add).then_inc(vals_made, 1)
                    hold(dve, vals_made, k + 1)
                    largest(top_val, group_val)
                if "u" in stages:
                    dve.wait_ge(y_made, upd + 1)
                    dve.wait_ge(x_upd_loaded[slot], in_slot(upd, slot) * 16)
                    wait(dve, x1_stored[slot], (in_slot(upd, slot) - 1) * 16)
                    dve.scalar_tensor_tensor(x1[:, slot, :], y_ps, 0.0, x_upd[:, slot, :], ALU.max,
                                             ALU.add).then_inc(x1_made, 1)
                if "n" in stages or "u" in stages:
                    if "n" in stages:
                        dve.wait_ge(x_norm_loaded[slot], in_slot(nrm - NORM_LEAD, slot) * 16)
                        last = dve.bn_stats(ln_stats[:, 0, :], x_norm[:, slot, :])
                    if "u" in stages:
                        dve.wait_ge(x1_made, upd + 1)
                        last = dve.bn_stats(ln_stats[:, 1, :], x1[:, slot, :])
                    own(last)
                    if "n" in stages:
                        last = dve.bn_aggr(ln_mv[:, 0, :], ln_stats[:, 0, :])
                    if "u" in stages:
                        last = dve.bn_aggr(ln_mv[:, 1, :], ln_stats[:, 1, :])
                    own(last)
                    if "n" in stages:
                        wait(dve, h_made, nrm - 1)
                    if "u" in stages:
                        wait(dve, h2_made, upd - 1)
                    c = slice(0 if "n" in stages else 1, 2 if "u" in stages else 1)
                    norm_scale(ln_scale[:, slot, c], c)
                    dve.scalar_tensor_tensor(ln_shift[:, slot, c], ln_mv[:, c, 0], -1.0, ln_scale[:, slot, c],
                                             ALU.mult, ALU.mult).then_inc(ln_shift_made, 1)
                if "p" in stages:
                    wide = [P, TOP, GROUP]
                    own(dve.tensor_copy(top_int[:], top_val[:]))
                    own(dve.tensor_scalar(top_col[:], top_int[:], 8, 3, ALU.logical_shift_right,
                                          ALU.logical_shift_left))
                    own(dve.tensor_tensor(nbr_bits[:], top_int[:].unsqueeze(2).broadcast_to(wide), group_bits[:],
                                          ALU.bitwise_and))
                    own(dve.tensor_tensor(col_keys[:], top_col[:].unsqueeze(2).broadcast_to(wide), group_off[:],
                                          ALU.subtract))
                    own(dve.scalar_tensor_tensor(keys[:, 0, :], nbr_bits[:].rearrange("p t o -> p (t o)"), 0,
                                                 col_keys[:].rearrange("p t o -> p (t o)"), ALU.not_equal, ALU.mult))
                    largest(top_keys, keys)
                    dve.tensor_scalar(picks[:, slot, :], top_keys[:, 0:PICKS], -1.0,
                                      table_base[:, bass.ds(k // TILES_PER_GRAPH, 1)], ALU.mult,
                                      ALU.add).then_inc(picks_made, 1)

            run_steps(dve, step)

        @block.scalar
        def _(act):
            act.wait_ge(first_shift_made, 1)
            for tile in range(NORM_LEAD):
                act.activation(first_h[:, tile, :], first_x[:, tile, :], ACT.Relu, bias=first_shift[:, tile:tile + 1],
                               scale=first_scale[:, tile:tile + 1]).then_inc(h_made, 1)
                if tile == TILES_PER_GRAPH:
                    act.wait_ge(zero_stored, 32)
                    for stored in h_stored:
                        act.wait_ge(stored, TILES_PER_GRAPH // 2 * 16)
                act.wait_ge(h_made, tile + 1)
                act.dma_start(table_tile(tile), first_h[:, tile, :]).then_inc(h_stored[tile % 2], 16)

            def step(k, slot, stages):
                nrm, upd, att, res = k + NORM_LEAD, k - UPDATE_LAG, k - ATTEND_LAG, k - RESULT_LAG
                if "p" in stages:
                    for half in range(2):
                        act.wait_ge(nbr_ps_made, k * 2 + half + 1)
                        if half == 0:
                            wait(act, byte_made, k)
                        act.activation(is_nbr_t[:, 8 * half:8 * half + 8, :], nbr_ps[half][:],
                                       ACT.Copy).then_inc(nbr_t_made, 1)
                if "a" in stages:
                    graph = att // TILES_PER_GRAPH
                    act.wait_ge(s2_made, (graph + 1) * TILES_PER_GRAPH)
                    wait(act, neg_max_made, att - 1)
                    act.activation(s1_cur[:, slot:slot + 1], s1[:, bass.ds(att % (2 * TILES_PER_GRAPH), 1)], ACT.Copy)
                    wait(act, masked_made, att)
                    act.activation(s2_cur[:], s2[:, bass.ds(graph % 2 * NODES, NODES)],
                                   ACT.Copy).then_inc(s2_cur_made, 1)
                    act.wait_ge(s2_cur_made, att + 1)
                    act.wait_ge(masked_made, att + 1)
                    act.activation(e[:, slot, :], e[:, slot, :], ACT.Identity,
                                   bias=s1_cur[:, slot:slot + 1]).then_inc(pre_made, 1)
                if "u" in stages:
                    act.wait_ge(ha_ps_made, upd + 1)
                    wait(act, y_made, upd)
                    act.activation(ha_t[:].rearrange("p j n -> p (j n)"), update_ps[:], ACT.Copy).then_inc(ha_t_made, 1)
                if "r" in stages:
                    act.wait_ge(result_made, res + 1)
                    act.dma_start(tile_rows(out_rows, res), result[:, 1 - slot, :]).then_inc(result_stored[1 - slot], 16)
                if "a" in stages:
                    act.wait_ge(neg_max_made, att + 1)
                    act.activation(e[:, slot, :], e[:, slot, :], ACT.Exp,
                                   bias=neg_max[:, slot:slot + 1]).then_inc(prob_made, 1)
                    for q in range(CHUNKS):
                        act.wait_ge(pt_ps_made, att * CHUNKS + q + 1)
                        if q == 0:
                            wait(act, att_made, att)
                        act.activation(prob_t[:, q, :, :], pt_ps[q % 2][:], ACT.Copy).then_inc(pt_made, 1)
                if "u" in stages:
                    act.wait_ge(ln_shift_made, k + 1)
                    wait(act, h2_ps_made, upd)
                    act.activation(h2[:], x1[:, slot, :], ACT.Relu, bias=ln_shift[:, slot, 1:2],
                                   scale=ln_scale[:, slot, 1:2]).then_inc(h2_made, 1)
                    act.dma_start(tile_rows(x1_rows, upd), x1[:, slot, :]).then_inc(x1_stored[slot], 16)
                    act.wait_ge(h2_ps_made, upd + 1)
                    wait(act, wh_ps_made, upd)
                    act.activation(h2_t[:].rearrange("p j n -> p (j n)"), update_ps[:, 0:2 * P],
                                   ACT.Copy).then_inc(h2_t_made, 1)
                if "n" in stages:
                    act.wait_ge(ln_shift_made, k + 1)
                    wait(act, h_stored[slot], (in_slot(nrm, slot) - 1) * 16)
                    act.activation(h_out[:, slot, :], x_norm[:, slot, :], ACT.Relu, bias=ln_shift[:, slot, 0:1],
                                   scale=ln_scale[:, slot, 0:1]).then_inc(h_made, 1)
                    act.wait_ge(h_made, nrm + 1)
                    act.dma_start(table_tile(nrm), h_out[:, slot, :]).then_inc(h_stored[slot], 16)
                if "u" in stages:
                    place = upd % (2 * TILES_PER_GRAPH)
                    act.wait_ge(wh_ps_made, upd + 1)
                    act.activation(wh[:, bass.ds(place, 1), 0:CH], wh_ps[:, 0:CH], ACT.Copy)
                    act.activation(s1[:, bass.ds(place, 1)], wh_ps[:, CH:CH + 1], ACT.Copy)
                    act.activation(s2[:, bass.ds(place * P, P)], s2_ps, ACT.Copy).then_inc(s2_made, 1)

            run_steps(act, step)

        @block.tensor
        def _(pe):
            pe.wait_ge(pool_made, 23)
            pe.wait_ge(weights_loaded, 64)
            pe.wait_ge(dve_consts_made, 8)

            def step(k, slot, stages):
                upd, att = k - UPDATE_LAG, k - ATTEND_LAG
                if "p" in stages:
                    pe.wait_ge(nbr_made, k + 1)
                    for half in range(2):
                        wait(pe, nbr_t_made, (k - 1) * 2 + half + 1)
                        for j in range(8):
                            col = (8 * half + j) * P
                            last = pe.transpose(nbr_ps[half][:, j, :], is_nbr[:, col:col + P], ident_b[:])
                        last.then_inc(nbr_ps_made, 1)
                    wait(pe, vals_made, k)
                    pe.wait_ge(nbr_t_made, k * 2 + 2)
                    width = P // GROUP
                    for j in range(TILES_PER_GRAPH):
                        last = pe.matmul(byte_ps[:, j * width:(j + 1) * width], is_nbr_t[:, j, :], byte_w[:],
                                         start=True, stop=True)
                    last.then_inc(byte_made, 1)
                if "u" in stages:
                    wait(pe, s2_made, upd)
                    pe.wait_ge(h_upd_loaded[slot], in_slot(upd, slot) * 16)
                    pe.wait_ge(agg_made, upd + 1)
                    for j in range(4):
                        half = (h_upd[:, slot, :] if j < 2 else agg[:])[:, j % 2 * P:(j % 2 + 1) * P]
                        last = pe.transpose(update_ps[:, j * P:(j + 1) * P], half, ident[:])
                    last.then_inc(ha_ps_made, 1)
                    pe.wait_ge(ha_t_made, upd + 1)
                    for j in range(4):
                        pe.matmul(y_ps, ha_t[:, j, :], w0_sb[:, j, :], start=j == 0, stop=False)
                    pe.matmul(y_ps, ones[0:1, :], b0_sb[:], start=False, stop=True).then_inc(y_made, 1)

                def transpose_chunk(q):
                    chunk = att * CHUNKS + q
                    wait(pe, pt_made, chunk - 1)
                    for j in range(4):
                        col = (4 * q + j) * P
                        last = pe.transpose(pt_ps[q % 2][:, j, :], e[:, slot, col:col + P], ident[:])
                    last.then_inc(pt_ps_made, 1)

                def multiply_chunk(q):
                    pe.wait_ge(pt_made, att * CHUNKS + q + 1)
                    for j in range(4):
                        node_tile = 4 * q + j
                        place = att // TILES_PER_GRAPH % 2 * TILES_PER_GRAPH + node_tile
                        last = pe.matmul(att_ps[:, 0:CH + 1], prob_t[:, q, j, :], wh[:, bass.ds(place, 1), :],
                                         start=node_tile == 0, stop=node_tile == TILES_PER_GRAPH - 1)
                    if q == CHUNKS - 1:
                        last.then_inc(att_made, 1)

                if "a" in stages:
                    pe.wait_ge(prob_made, att + 1)
                    transpose_chunk(0)
                    wait(pe, result_made, att)
                    pe.wait_ge(s2_made, (att // TILES_PER_GRAPH + 1) * TILES_PER_GRAPH)
                    for q in range(1, CHUNKS):
                        transpose_chunk(q)
                        multiply_chunk(q - 1)
                    multiply_chunk(CHUNKS - 1)
                if "u" in stages:
                    pe.wait_ge(h2_made, upd + 1)
                    for j in range(2):
                        last = pe.transpose(update_ps[:, j * P:(j + 1) * P], h2[:, j * P:(j + 1) * P], ident[:])
                    last.then_inc(h2_ps_made, 1)
                    pe.wait_ge(h2_t_made, upd + 1)
                    for j in range(2):
                        pe.matmul(wh_ps, h2_t[:, j, :], w1s[:, j, :], start=j == 0, stop=j == 1)
                    for j in range(2):
                        last = pe.matmul(s2_ps, w2_bc[:, j, :], h2_t[:, j, :], start=j == 0, stop=j == 1)
                    last.then_inc(wh_ps_made, 1)

            run_steps(pe, step)


_INS = ["x", "adj", "L0_gnn_W", "L0_gnn_b", "L1_gnn_W", "L1_gnn_a"]


def kernel(**inputs):
    import numpy as np
    import concourse.bacc as bacc
    from concourse.bass_utils import run_bass_kernel_spmd

    nc = bacc.Bacc("TRN2", target_bir_lowering=False, num_devices=1)
    arrays, args = {}, []
    for name in _INS:
        array = np.ascontiguousarray(inputs[name])
        arrays[name] = array
        args.append(nc.dram_tensor(name, array.shape, mybir.dt.from_np(array.dtype), kind="ExternalInput").ap())
    out = nc.dram_tensor("out", (GRAPHS, NODES, CH), mybir.dt.float32, kind="ExternalOutput").ap()
    graph_layers(nc, *args, out)
    ran = run_bass_kernel_spmd(nc, [arrays], core_ids=[0])
    return ran.results[0]["out"]
```

```python
from contextlib import ExitStack

import concourse.bass as bass
from concourse import mybir

P = 128
GRAPHS, NODES, CH = 8, 2048, 256
PICKS = 25
TILES_PER_GRAPH = NODES // P
TILES = GRAPHS * TILES_PER_GRAPH
TABLE_ROWS = NODES + 1
TABLE_GRAPHS = 3
ZERO_RUN = TABLE_ROWS * CH // P
ROUNDS = (PICKS + 7) // 8
GROUP = 8
GROUPS = NODES // GROUP
TOP = 8 * ROUNDS
NORM_LEAD, UPDATE_LAG, MASK_LAG, ATTEND_LAG, MULTIPLY_LAG, RESULT_LAG = 18, 2, 17, 18, 19, 20
LN_EPS = 1e-5
NEWTON_STEPS = 3
ROOT_PARTS = 2 + 3 * NEWTON_STEPS
NORM_PARTS = ROOT_PARTS + 3
KEY_PARTS = 5 + 2 * ROUNDS
ROOT_GUESS = 0x5F3759DF
LEAKY_SLOPE = 0.2
NEG_BIG = -9e15
CHUNKS = NODES // 512

PHASES = [
    (0, 2, "nbpf", "nbpf"),
    (2, 4, "nbpfuh", "nbpfuh"),
    (4, 16, "nbpfuh", "nbpfuh"),
    (16, 18, "nbpuh", "nbpuho"),
    (18, 20, "nbpuoca", "nbpuocam"),
    (20, 22, "nbpuocamr", "nbpuocamr"),
    (22, 110, "nbpuocamr", "nbpuocamr"),
    (110, 126, "bpuocamr", "bpuocamr"),
    (126, 128, "bpuocamr", "puocamr"),
    (128, 130, "uocamr", "uocamr"),
    (130, 132, "ocamr", "oamr"),
    (132, 144, "oamr", "oamr"),
    (144, 146, "oamr", "amr"),
    (146, 148, "mr", "r"),
]


def run_steps(eng, body):
    for first, end, even, odd in PHASES:
        if end - first == 2:
            body(first, 0, even)
            body(first + 1, 1, odd)
            continue
        with eng.Fori(0, (end - first) // 2) as pair:
            body(pair * 2 + first, 0, even)
            body(pair * 2 + (first + 1), 1, odd)


def wait(eng, sem, count):
    if not isinstance(count, int) or count > 0:
        eng.wait_ge(sem, count)


def hold(eng, sem, count):
    eng.wait_ge(sem, count)
    eng.nop(nofuse=True)


def at(step, *places):
    return isinstance(step, int) and step in places


def in_slot(tile, slot):
    return (tile - slot) // 2 + 1


def graph_layers(nc, x, adj, w0, b0, w1, a1, out):
    fp32, bf16 = mybir.dt.float32, mybir.dt.bfloat16
    i32, u32 = mybir.dt.int32, mybir.dt.uint32
    ALU = mybir.AluOpType
    ACT = mybir.ActivationFunctionType
    AX = mybir.AxisListType

    x_rows = x.rearrange("g n c -> (g n) c")
    adj_rows = adj.rearrange("g n m -> (g n) m")
    out_rows = out.rearrange("g n c -> (g n) c")
    table = nc.dram_tensor("table", [TABLE_GRAPHS * TABLE_ROWS, CH], fp32, kind="Internal").ap()
    first_table = nc.dram_tensor("first_table", [TABLE_ROWS, CH], fp32, kind="Internal").ap()
    x1_rows = nc.dram_tensor("x1_rows", [GRAPHS * NODES, CH], fp32, kind="Internal").ap()

    def tile_rows(rows, tile):
        return rows[bass.ds(tile * P, P), :]

    def table_tile(tile):
        graph_slot = tile // TILES_PER_GRAPH % TABLE_GRAPHS
        return table[bass.ds(graph_slot * TABLE_ROWS + tile % TILES_PER_GRAPH * P, P), :]

    with ExitStack() as ctx:
        def sb(name, shape, dt=fp32):
            return ctx.enter_context(nc.sbuf_tensor(name, shape, dt))

        def ps(name, shape, dt=fp32):
            return ctx.enter_context(nc.psum_tensor(name, shape, dt))

        def sem(name):
            return ctx.enter_context(nc.semaphore(name))

        def sem2(name):
            return [sem(f"{name}{i}") for i in range(2)]

        ident = sb("ident", [P, P])
        ident_b = sb("ident_b", [P, P], bf16)
        ones = sb("ones", [P, P])
        byte_w = sb("byte_w", [P, P // GROUP], bf16)
        group_base = sb("group_base", [P, GROUPS])
        group_bits = sb("group_bits", [P, TOP, GROUP], i32)
        group_off = sb("group_off", [P, TOP, GROUP], i32)
        table_base = sb("table_base", [P, 9])
        w0_sb = sb("w0_sb", [P, 4, CH])
        b0_sb = sb("b0_sb", [1, CH])
        w1s = sb("w1s", [P, 2, CH + 1])
        wa = sb("wa", [P, 4])
        w2_bc = sb("w2_bc", [P, 2, P])
        ln_stats = sb("ln_stats", [P, NORM_LEAD, 6])
        ln_mv = sb("ln_mv", [P, NORM_LEAD, 2])
        ln_var = sb("ln_var", [P, NORM_LEAD])
        ln_root = sb("ln_root", [P, NORM_LEAD])
        ln_err = sb("ln_err", [P, NORM_LEAD])
        ln_scale = sb("ln_scale", [P, 2, 2])
        ln_shift = sb("ln_shift", [P, 2, 2])
        first_scale = sb("first_scale", [P, NORM_LEAD])
        first_shift = sb("first_shift", [P, NORM_LEAD])
        x_norm = sb("x_norm", [P, 2, CH])
        h_out = sb("h_out", [P, 2, CH])
        adj_pick = sb("adj_pick", [P, NODES], i32)
        nbr_sign = sb("nbr_sign", [P, NODES], bf16)
        is_nbr_t = sb("is_nbr_t", [P, TILES_PER_GRAPH, P], bf16)
        group_val = sb("group_val", [P, 2, GROUPS])
        top_val = sb("top_val", [P, TOP])
        top_int = sb("top_int", [P, TOP], i32)
        top_col = sb("top_col", [P, TOP], i32)
        nbr_bits = sb("nbr_bits", [P, TOP, GROUP], i32)
        col_keys = sb("col_keys", [P, TOP, GROUP])
        keys = sb("keys", [P, 2, TOP * GROUP])
        top_keys = sb("top_keys", [P, TOP])
        picks = sb("picks", [P, 2, PICKS], u32)
        rows = sb("rows", [P, 2, PICKS * CH])
        x_upd = sb("x_upd", [P, 2, CH])
        h_upd = sb("h_upd", [P, 2, CH])
        agg = sb("agg", [P, CH])
        ha_t = sb("ha_t", [P, 4, P])
        x1 = sb("x1", [P, 2, CH])
        h2 = sb("h2", [P, CH])
        h2_t = sb("h2_t", [P, 2, P])
        wh = sb("wh", [P, 2 * TILES_PER_GRAPH, CH + 1])
        s1 = sb("s1", [P, 2 * TILES_PER_GRAPH])
        s2 = sb("s2", [P, 2 * NODES])
        adj_att = sb("adj_att", [P, NODES], i32)
        off_mask = sb("off_mask", [P, NODES], bf16)
        s2_cur = sb("s2_cur", [P, NODES])
        row_max = sb("row_max", [P, 1])
        e = sb("e", [P, 2, NODES])
        neg_pre = sb("neg_pre", [P, 1])
        neg_max = sb("neg_max", [P, 2])
        prob_t = sb("prob_t", [P, CHUNKS, 4, P])
        inv_sum = sb("inv_sum", [P, 1])
        x1_att = sb("x1_att", [P, 2, CH])
        result = sb("result", [P, 2, CH])

        zeros = wh[:].rearrange("p t c -> p (t c)")[:, 0:ZERO_RUN]
        first_x = rows[:, 0, 0:NORM_LEAD * CH].rearrange("p (t c) -> p t c", c=CH)
        first_h = rows[:, 1, 0:NORM_LEAD * CH].rearrange("p (t c) -> p t c", c=CH)
        a_bc, a_prod = e[:, 0, 0:2 * CH], e[:, 0, 2 * CH:3 * CH]
        ident_zero = e[:, 1, 0:P]
        group_base_i = adj_att[:, 0:GROUPS]
        table_base_i = adj_att[:, GROUPS:GROUPS + 9]

        update_ps = ps("update_ps", [P, 512])
        y_ps, wh_ps, s2_ps = update_ps[:, 0:CH], update_ps[:, 0:CH + 1], update_ps[:, CH + 128:CH + 256]
        nbr_ps = [ps(f"nbr_ps{i}", [P, 8, P], bf16) for i in range(2)]
        byte_ps = ps("byte_ps", [P, 512])
        pt_ps = [ps(f"pt_ps{i}", [P, 4, P]) for i in range(2)]
        att_ps = ps("att_ps", [P, 512])

        weights_loaded, x_first_loaded = sem("weights_loaded"), [sem(f"x_first_loaded{i}") for i in range(3)]
        pool_made, dve_consts_made = sem("pool_made"), sem("dve_consts_made")
        ident_made, first_shift_made = sem("ident_made"), sem("first_shift_made")
        zeros_made, zero_row_stored, zero_stored = sem("zeros_made"), sem("zero_row_stored"), sem("zero_stored")
        x_norm_loaded, adj_pick_loaded, x_upd_loaded = sem2("x_norm_loaded"), sem("adj_pick_loaded"), sem2("x_upd_loaded")
        h_upd_loaded, adj_att_loaded, x1_att_loaded = sem2("h_upd_loaded"), sem("adj_att_loaded"), sem2("x1_att_loaded")
        rows_loaded = sem2("rows_loaded")
        h_stored, x1_stored, result_stored = sem2("h_stored"), sem2("x1_stored"), sem2("result_stored")
        dve_done = sem("dve_done")
        ln_shift_made, h_made = sem("ln_shift_made"), sem("h_made")
        nbr_made, nbr_ps_made, nbr_t_made, byte_made = sem("nbr_made"), sem("nbr_ps_made"), sem("nbr_t_made"), sem("byte_made")
        vals_made, picks_made = sem("vals_made"), sem("picks_made")
        agg_made, ha_ps_made, ha_t_made, y_made = sem("agg_made"), sem("ha_ps_made"), sem("ha_t_made"), sem("y_made")
        x1_made, h2_made, h2_ps_made, h2_t_made = sem("x1_made"), sem("h2_made"), sem("h2_ps_made"), sem("h2_t_made")
        wh_ps_made, s2_made = sem("wh_ps_made"), sem("s2_made")
        s2_cur_made, mask_made, masked_made = sem("s2_cur_made"), sem("mask_made"), sem("masked_made")
        pre_made, neg_max_made, prob_made = sem("pre_made"), sem("neg_max_made"), sem("prob_made")
        pt_ps_made, pt_made, att_made = sem("pt_ps_made"), sem("pt_made"), sem("att_made")
        result_made = sem("result_made")

        block = ctx.enter_context(nc.Block())

        @block.sync
        def _(sp):
            third = NORM_LEAD // 3
            for i, loaded in enumerate(x_first_loaded):
                sp.dma_start(first_x[:, i * third:(i + 1) * third, :],
                             x_rows[i * third * P:(i + 1) * third * P, :].rearrange("(t p) c -> p t c", p=P)
                             ).then_inc(loaded, 16)
            sp.dma_start(adj_pick[:], tile_rows(adj_rows, 0)).then_inc(adj_pick_loaded, 16)

            def first_transfers():
                sp.wait_ge(zeros_made, 1)
                for tables_row in (first_table[NODES:TABLE_ROWS, :], table[2 * TABLE_ROWS - 1:2 * TABLE_ROWS, :]):
                    sp.dma_start(tables_row, zeros[0:1, 0:CH]).then_inc(zero_row_stored, 16)
                for tile in range(TILES_PER_GRAPH):
                    sp.wait_ge(h_made, tile + 1)
                    sp.dma_start(tile_rows(first_table, tile), first_h[:, tile, :]).then_inc(h_stored[tile % 2], 16)
                sp.dma_start(w1s[:, :, 0:CH], w1.rearrange("(k p) o -> p k o", p=P)).then_inc(weights_loaded, 16)
                sp.dma_start(a_bc, a1.rearrange("n a -> a n").broadcast_to([P, 2 * CH])).then_inc(weights_loaded, 16)
                sp.dma_start(w0_sb[:], w0.rearrange("(k p) o -> p k o", p=P)).then_inc(weights_loaded, 16)
                sp.dma_start(b0_sb[:], b0.rearrange("(a n) -> a n", a=1)).then_inc(weights_loaded, 16)

            def second_transfers():
                for stored in h_stored:
                    sp.wait_ge(stored, TILES_PER_GRAPH // 2 * 16)
                for tile in range(TILES_PER_GRAPH, NORM_LEAD):
                    sp.wait_ge(h_made, tile + 1)
                    sp.dma_start(table_tile(tile), first_h[:, tile, :]).then_inc(h_stored[tile % 2], 16)
                for graph in (0, 2):
                    slot_rows = table[graph * TABLE_ROWS:(graph + 1) * TABLE_ROWS, :].rearrange("r c -> (r c)")
                    sp.dma_start(slot_rows.rearrange("(p f) -> p f", p=P), zeros).then_inc(zero_stored, 16)

            def step(k, slot, stages):
                nrm, upd, mask, mul = k + NORM_LEAD, k - UPDATE_LAG, k - MASK_LAG, k - MULTIPLY_LAG
                if "b" in stages:
                    sp.wait_ge(nbr_made, k + 1)
                    sp.dma_start(adj_pick[:], tile_rows(adj_rows, k + 1)).then_inc(adj_pick_loaded, 16)
                if "o" in stages:
                    wait(sp, mask_made, mask)
                    sp.dma_start(adj_att[:], tile_rows(adj_rows, mask)).then_inc(adj_att_loaded, 16)
                if "u" in stages:
                    wait(sp, x1_made, upd - 1)
                    sp.dma_start(x_upd[:, slot, :], tile_rows(x_rows, upd)).then_inc(x_upd_loaded[slot], 16)
                    wait(sp, ha_ps_made, upd - 1)
                    wait(sp, h_stored[slot], in_slot(upd, slot) * 16)
                    h_rows = tile_rows(first_table, upd) if "h" in stages else table_tile(upd)
                    sp.dma_start(h_upd[:, slot, :], h_rows).then_inc(h_upd_loaded[slot], 16)
                if "n" in stages:
                    if not at(k, 0, 1):
                        wait(sp, h_made, nrm - 1)
                    sp.dma_start(x_norm[:, slot, :], tile_rows(x_rows, nrm)).then_inc(x_norm_loaded[slot], 16)
                if "m" in stages:
                    wait(sp, result_made, mul - 1)
                    wait(sp, x1_stored[1 - slot], in_slot(mul, 1 - slot) * 16)
                    sp.dma_start(x1_att[:, 1 - slot, :], tile_rows(x1_rows, mul)).then_inc(x1_att_loaded[1 - slot], 16)
                if at(k, 0):
                    first_transfers()
                if at(k, 1):
                    second_transfers()

            run_steps(sp, step)
            for stored in (*h_stored, *x1_stored, *result_stored):
                sp.wait_ge(stored, TILES // 2 * 16)
            sp.wait_ge(zero_stored, 32)

        @block.gpsimd
        def _(pool):
            pool.memset(ident_zero, 0.0).then_inc(pool_made, 1)
            pool.memset(ones[:], 1.0).then_inc(pool_made, 1)
            pool.memset(byte_w[:], 0.0).then_inc(pool_made, 1)
            pool.iota(group_base_i, [[-GROUPS, GROUPS]], base=GROUPS * GROUPS,
                      channel_multiplier=0).then_inc(pool_made, 1)
            pool.iota(table_base_i, [[0, 3], [TABLE_ROWS, TABLE_GRAPHS]], base=NODES,
                      channel_multiplier=0).then_inc(pool_made, 1)
            pool.iota(group_off[:], [[0, TOP], [1, GROUP]], base=0, channel_multiplier=0).then_inc(pool_made, 1)
            for o in range(GROUP):
                pool.memset(group_bits[:, :, o:o + 1], 1 << (GROUP - 1 - o)).then_inc(pool_made, 1)
            pool.wait_ge(pool_made, 14)
            pool.affine_select(out=ident[:], in_=ident_zero, compare_op=ALU.not_equal, fill=1.0, base=0,
                               pattern=[[-1, P]], channel_multiplier=1).then_inc(pool_made, 1)
            for o in range(GROUP):
                pool.affine_select(out=byte_w[:], in_=byte_w[:], compare_op=ALU.not_equal,
                                   fill=float(1 << (GROUP - 1 - o)), base=-o,
                                   pattern=[[-GROUP, P // GROUP]], channel_multiplier=1).then_inc(pool_made, 1)
                pool.wait_ge(pool_made, 16 + o)
            pool.memset(zeros, 0.0).then_inc(zeros_made, 1)

            def step(k, slot, stages):
                if "p" in stages:
                    graph = k // TILES_PER_GRAPH
                    for stored in h_stored:
                        pool.wait_ge(stored, (graph + 1) * (TILES_PER_GRAPH // 2 * 16))
                    if at(k, 0):
                        pool.wait_ge(zero_row_stored, 32)
                        pool.wait_ge(h_made, NORM_LEAD)
                    if at(k, TILES_PER_GRAPH):
                        pool.wait_ge(zero_stored, 32)
                    if at(k, 1):
                        for stored in h_stored:
                            pool.wait_ge(stored, NORM_LEAD // 2 * 16)
                    wait(pool, agg_made, k - 1)
                    hold(pool, picks_made, k + 1)
                    for i in range(PICKS):
                        pool.indirect_dma_start(
                            out=rows[:, slot, i * CH:(i + 1) * CH], out_offset=None,
                            in_=first_table if "f" in stages else table,
                            in_offset=bass.IndirectOffsetOnAxis(ap=picks[:, slot, i:i + 1], axis=0),
                        ).then_inc(rows_loaded[slot], 16)

            run_steps(pool, step)

        @block.vector
        def _(dve):
            dones = [0]

            def done(instruction):
                instruction.then_inc(dve_done, 1)
                dones[0] += 1
                return dones[0]

            def after(count):
                dve.wait_ge(dve_done, count)

            def restart():
                after(dones[0])
                dve.sem_clear(dve_done)
                dones[0] = 0

            def norm_root(part, scale, columns):
                var, root, err = ln_var[:, columns], ln_root[:, columns], ln_err[:, columns]
                if part == 0:
                    return dve.tensor_scalar(var, ln_mv[:, columns, 1], LN_EPS, None, ALU.add)
                if part == 1:
                    return dve.tensor_scalar(root.bitcast(i32), var.bitcast(i32), -0.5, float(ROOT_GUESS),
                                             ALU.mult, ALU.add)
                if part % 3 == 2:
                    return dve.tensor_tensor(err, root, root, ALU.mult)
                if part % 3 == 0:
                    return dve.scalar_tensor_tensor(err, err, -0.5, var, ALU.mult, ALU.mult)
                return dve.scalar_tensor_tensor(scale if part == ROOT_PARTS - 1 else root, err, 1.5, root,
                                                ALU.add, ALU.mult)

            for tile in range(NORM_LEAD):
                if tile % (NORM_LEAD // 3) == 0:
                    dve.wait_ge(x_first_loaded[tile // (NORM_LEAD // 3)], 16)
                last = dve.bn_stats(ln_stats[:, tile, :], first_x[:, tile, :])
            done(last)
            dve.wait_ge(pool_made, 23)
            dve.tensor_copy(group_base[:], group_base_i).then_inc(dve_consts_made, 1)
            dve.tensor_copy(table_base[:], table_base_i).then_inc(dve_consts_made, 1)
            dve.tensor_copy(ident_b[:], ident[:]).then_inc(dve_consts_made, 1)
            dve.wait_ge(dve_consts_made, 3)
            restart()

            def first_norm():
                for tile in range(NORM_LEAD):
                    last = dve.bn_aggr(ln_mv[:, tile, :], ln_stats[:, tile, :])
                after(done(last))
                for part in range(ROOT_PARTS):
                    after(done(norm_root(part, first_scale[:], slice(0, NORM_LEAD))))
                dve.scalar_tensor_tensor(first_shift[:], ln_mv[:, :, 0], -1.0, first_scale[:], ALU.mult,
                                         ALU.mult).then_inc(first_shift_made, 1)

            def weight_constants():
                dve.wait_ge(weights_loaded, 64)
                for half in range(2):
                    for k in range(2):
                        n = 2 * half + k
                        after(done(dve.tensor_tensor(a_prod, w1s[:, k, 0:CH], a_bc[:, half * CH:(half + 1) * CH], ALU.mult)))
                        after(done(dve.tensor_reduce(out=wa[:, n:n + 1], in_=a_prod, axis=AX.X, op=ALU.add)))
                for k in range(2):
                    dve.tensor_copy(w1s[:, k, CH:CH + 1], wa[:, k:k + 1]).then_inc(dve_consts_made, 1)
                    dve.tensor_scalar(w2_bc[:, k, :], ones[:], wa[:, 2 + k:3 + k], None,
                                      ALU.mult).then_inc(dve_consts_made, 1)
                dve.wait_ge(dve_consts_made, 7)

            def step(k, slot, stages):
                nrm, upd, mask = k + NORM_LEAD, k - UPDATE_LAG, k - MASK_LAG
                att, res = k - ATTEND_LAG, k - RESULT_LAG
                if at(k, 0):
                    first_norm()

                def maximum(part):
                    quarter = slice(part * CH // 4, (part + 1) * CH // 4)
                    return dve.tensor_reduce(
                        out=agg[:, quarter], in_=rows[:, slot, :].rearrange("p (k c) -> p c k", c=CH)[:, quarter, :],
                        axis=AX.X, op=ALU.max)

                def group_round(part):
                    n = part // 2
                    eight, now, then = top_val[:, 8 * n:8 * n + 8], group_val[:, n % 2, :], group_val[:, 1 - n % 2, :]
                    if part % 2 == 0:
                        return done(dve.max(eight, now))
                    return done(dve.match_replace(then, eight, now, 0.0))

                def make_mask():
                    dve.wait_ge(adj_att_loaded, (mask + 1) * 16)
                    wait(dve, masked_made, mask)
                    dve.tensor_scalar(off_mask[:], adj_att[:], 0, NEG_BIG, ALU.is_le,
                                      ALU.mult).then_inc(mask_made, 1)

                if "p" in stages:
                    dve.wait_ge(byte_made, k + 1)
                    after(done(dve.scalar_tensor_tensor(group_val[:, 1, :], byte_ps[:, 0:GROUPS], 0.0, group_base[:],
                                                        ALU.is_gt, ALU.mult)))
                    dve.tensor_tensor(group_val[:, 0, :], group_val[:, 1, :], byte_ps[:, 0:GROUPS],
                                      ALU.add).then_inc(vals_made, 1)
                    hold(dve, vals_made, k + 1)
                    grouped = group_round(0)
                if "u" in stages:
                    dve.wait_ge(rows_loaded[slot], in_slot(upd, slot) * (PICKS * 16))
                    wait(dve, ha_ps_made, upd)
                    maximum(0)
                if "p" in stages:
                    after(grouped)
                    grouped = group_round(1)
                if "u" in stages:
                    maximum(1)
                if "p" in stages:
                    after(grouped)
                    grouped = group_round(2)
                if "u" in stages:
                    maximum(2)
                    maximum(3).then_inc(agg_made, 1)
                if "a" in stages:
                    dve.wait_ge(mask_made, att + 1)
                    wait(dve, pt_ps_made, (att - 1) * CHUNKS)
                    if "c" in stages:
                        dve.wait_ge(s2_cur_made, att + 1)
                    dve.nop(nofuse=True)
                    dve.tensor_tensor_reduce(out=e[:, slot, :], in0=s2_cur[:], in1=off_mask[:], scale=1.0,
                                             scalar=-3.0e38, op0=ALU.add, op1=ALU.max,
                                             accum_out=row_max[:]).then_inc(masked_made, 1)
                if "p" in stages:
                    after(grouped)
                    grouped = group_round(3)
                if "o" in stages:
                    make_mask()
                if "p" in stages:
                    after(grouped)
                    grouped = group_round(4)
                if "a" in stages:
                    dve.wait_ge(masked_made, att + 1)
                    pre = done(dve.tensor_scalar(neg_pre[:], row_max[:], s1[:, bass.ds(att % (2 * TILES_PER_GRAPH), 1)],
                                                 -1.0, ALU.add, ALU.mult))
                if "r" in stages:
                    dve.wait_ge(att_made, res + 1)
                    inv = done(dve.reciprocal(inv_sum[:], att_ps[:, CH:CH + 1]))
                if "p" in stages:
                    after(grouped)
                    grouped = group_round(5)
                if "r" in stages:
                    dve.wait_ge(x1_att_loaded[slot], in_slot(res, slot) * 16)
                    wait(dve, result_stored[slot], (in_slot(res, slot) - 1) * 16)
                    after(inv)
                    dve.scalar_tensor_tensor(result[:, slot, :], att_ps[:, 0:CH], inv_sum[:], x1_att[:, slot, :],
                                             ALU.mult, ALU.add).then_inc(result_made, 1)
                if "p" in stages:
                    after(grouped)
                    grouped = group_round(2 * ROUNDS - 2)
                if "n" in stages:
                    dve.wait_ge(x_norm_loaded[slot], in_slot(nrm - NORM_LEAD, slot) * 16)
                    if not at(k, 0, 1):
                        wait(dve, h_made, nrm - 1)
                    stats = done(dve.bn_stats(ln_stats[:, 0, :], x_norm[:, slot, :]))
                if "u" in stages:
                    dve.wait_ge(y_made, upd + 1)
                    dve.wait_ge(x_upd_loaded[slot], in_slot(upd, slot) * 16)
                    wait(dve, x1_stored[slot], (in_slot(upd, slot) - 1) * 16)
                    dve.scalar_tensor_tensor(x1[:, slot, :], y_ps, 0.0, x_upd[:, slot, :], ALU.max,
                                             ALU.add).then_inc(x1_made, 1)
                    wait(dve, h2_made, upd - 1)

                def leaky():
                    dve.wait_ge(pre_made, att + 1)
                    dve.scalar_tensor_tensor(e[:, slot, :], e[:, slot, :], LEAKY_SLOPE, e[:, slot, :], ALU.mult, ALU.max)
                    wait(dve, prob_made, att - 1)
                    after(pre)
                    dve.scalar_tensor_tensor(neg_max[:, slot:slot + 1], neg_pre[:], LEAKY_SLOPE, neg_pre[:], ALU.mult,
                                             ALU.min).then_inc(neg_max_made, 1)

                c = slice(0 if "n" in stages else 1, 2 if "u" in stages else 1)
                last_norm = last_key = 0

                def norm_part(part):
                    if part == 0:
                        if "u" not in stages:
                            return stats
                        dve.wait_ge(x1_made, upd + 1)
                        return done(dve.bn_stats(ln_stats[:, 1, :], x1[:, slot, :]))
                    after(last_norm)
                    if part == 1:
                        if "n" in stages:
                            last = dve.bn_aggr(ln_mv[:, 0, :], ln_stats[:, 0, :])
                        if "u" in stages:
                            last = dve.bn_aggr(ln_mv[:, 1, :], ln_stats[:, 1, :])
                        return done(last)
                    if part < NORM_PARTS - 1:
                        return done(norm_root(part - 2, ln_scale[:, slot, c], c))
                    dve.scalar_tensor_tensor(ln_shift[:, slot, c], ln_mv[:, c, 0], -1.0, ln_scale[:, slot, c],
                                             ALU.mult, ALU.mult).then_inc(ln_shift_made, 1)

                def key_part(part):
                    wide = [P, TOP, GROUP]
                    after(last_key)
                    if part == 0:
                        return done(dve.tensor_copy(top_int[:], top_val[:]))
                    if part == 1:
                        return done(dve.tensor_scalar(top_col[:], top_int[:], 8, 3, ALU.logical_shift_right,
                                                      ALU.logical_shift_left))
                    if part == 2:
                        return done(dve.tensor_tensor(nbr_bits[:], top_int[:].unsqueeze(2).broadcast_to(wide),
                                                      group_bits[:], ALU.bitwise_and))
                    if part == 3:
                        return done(dve.tensor_tensor(col_keys[:], top_col[:].unsqueeze(2).broadcast_to(wide),
                                                      group_off[:], ALU.subtract))
                    if part == 4:
                        return done(dve.scalar_tensor_tensor(
                            keys[:, 0, :], nbr_bits[:].rearrange("p t o -> p (t o)"), 0,
                            col_keys[:].rearrange("p t o -> p (t o)"), ALU.not_equal, ALU.mult))
                    if part < KEY_PARTS - 1:
                        n = (part - 5) // 2
                        eight, now, then = top_keys[:, 8 * n:8 * n + 8], keys[:, n % 2, :], keys[:, 1 - n % 2, :]
                        if part % 2 == 1:
                            return done(dve.max(eight, now))
                        return done(dve.match_replace(then, eight, now, 0.0))
                    dve.tensor_scalar(picks[:, slot, :], top_keys[:, 0:PICKS], -1.0,
                                      table_base[:, bass.ds(k // TILES_PER_GRAPH, 1)], ALU.mult,
                                      ALU.add).then_inc(picks_made, 1)

                if "p" in stages:
                    last_key = grouped
                leaky_after = NORM_PARTS - 1 if "u" in stages and "p" not in stages else 0
                for part in range(max(NORM_PARTS, KEY_PARTS)):
                    if part < KEY_PARTS and "p" in stages:
                        last_key = key_part(part)
                    if part < NORM_PARTS and ("n" in stages or "u" in stages):
                        last_norm = norm_part(part)
                    if part == leaky_after and "a" in stages:
                        leaky()
                if at(k, 0):
                    weight_constants()
                if at(k, 1):
                    dve.wait_ge(zero_stored, 32)
                    dve.memset(wh[:, :, CH:CH + 1], 1.0).then_inc(dve_consts_made, 1)
                restart()

            run_steps(dve, step)

        @block.scalar
        def _(act):
            def first_tiles():
                act.wait_ge(first_shift_made, 1)
                for tile in range(NORM_LEAD):
                    act.activation(first_h[:, tile, :], first_x[:, tile, :], ACT.Relu,
                                   bias=first_shift[:, tile:tile + 1],
                                   scale=first_scale[:, tile:tile + 1]).then_inc(h_made, 1)

            def make_sign(tile):
                act.wait_ge(adj_pick_loaded, (tile + 1) * 16)
                wait(act, nbr_ps_made, tile * 2)
                act.activation(nbr_sign[:], adj_pick[:], ACT.Sign).then_inc(nbr_made, 1)

            def square_sign(tile):
                for half in range(2):
                    act.wait_ge(nbr_ps_made, tile * 2 + half + 1)
                    if half == 0:
                        wait(act, byte_made, tile)
                    act.activation(is_nbr_t[:, 8 * half:8 * half + 8, :], nbr_ps[half][:],
                                   ACT.Square).then_inc(nbr_t_made, 1)

            def step(k, slot, stages):
                nrm, upd, att = k + NORM_LEAD, k - UPDATE_LAG, k - ATTEND_LAG
                mul, res = k - MULTIPLY_LAG, k - RESULT_LAG
                if at(k, UPDATE_LAG):
                    act.wait_ge(zero_stored, 32)
                if at(k, 0):
                    make_sign(0)
                    square_sign(0)
                    first_tiles()
                if "c" in stages:
                    graph = att // TILES_PER_GRAPH
                    act.wait_ge(s2_made, (graph + 1) * TILES_PER_GRAPH)
                    wait(act, masked_made, att)
                    act.activation(s2_cur[:], s2[:, bass.ds(graph % 2 * NODES, NODES)],
                                   ACT.Copy).then_inc(s2_cur_made, 1)

                if "b" in stages:
                    make_sign(k + 1)

                def copy_chunk(q):
                    act.wait_ge(pt_ps_made, mul * CHUNKS + q + 1)
                    if q == 0:
                        wait(act, att_made, mul)
                    act.activation(prob_t[:, q, :, :], pt_ps[q % 2][:], ACT.Copy).then_inc(pt_made, 1)

                def add_s1():
                    act.wait_ge(masked_made, att + 1)
                    act.activation(e[:, slot, :], e[:, slot, :], ACT.Identity,
                                   bias=s1[:, bass.ds(att % (2 * TILES_PER_GRAPH), 1)]).then_inc(pre_made, 1)

                if "u" in stages:
                    act.wait_ge(ha_ps_made, upd + 1)
                    wait(act, y_made, upd)
                    act.activation(ha_t[:].rearrange("p j n -> p (j n)"), update_ps[:], ACT.Copy).then_inc(ha_t_made, 1)
                if "u" not in stages and "a" in stages:
                    add_s1()
                if "m" in stages:
                    copy_chunk(0)
                    copy_chunk(1)
                if "u" in stages and "a" in stages:
                    add_s1()
                if "m" in stages:
                    copy_chunk(2)
                    copy_chunk(3)
                if "b" in stages:
                    square_sign(k + 1)

                def exponentials():
                    act.wait_ge(neg_max_made, att + 1)
                    act.activation(e[:, slot, :], e[:, slot, :], ACT.Exp,
                                   bias=neg_max[:, slot:slot + 1]).then_inc(prob_made, 1)

                late = "u" in stages and "p" not in stages
                if "a" in stages and not late:
                    exponentials()
                if "r" in stages:
                    act.wait_ge(result_made, res + 1)
                    act.dma_start(tile_rows(out_rows, res), result[:, slot, :]).then_inc(result_stored[slot], 16)
                if "u" in stages:
                    act.wait_ge(ln_shift_made, k + 1)
                    wait(act, h2_ps_made, upd)
                    act.activation(h2[:], x1[:, slot, :], ACT.Relu, bias=ln_shift[:, slot, 1:2],
                                   scale=ln_scale[:, slot, 1:2]).then_inc(h2_made, 1)
                    act.dma_start(tile_rows(x1_rows, upd), x1[:, slot, :]).then_inc(x1_stored[slot], 16)
                    act.wait_ge(h2_ps_made, upd + 1)
                    wait(act, wh_ps_made, upd)
                    act.activation(h2_t[:].rearrange("p j n -> p (j n)"), update_ps[:, 0:2 * P],
                                   ACT.Copy).then_inc(h2_t_made, 1)
                if "n" in stages:
                    act.wait_ge(ln_shift_made, k + 1)
                    wait(act, h_stored[slot], (in_slot(nrm, slot) - 1) * 16)
                    act.activation(h_out[:, slot, :], x_norm[:, slot, :], ACT.Relu, bias=ln_shift[:, slot, 0:1],
                                   scale=ln_scale[:, slot, 0:1]).then_inc(h_made, 1)
                    act.wait_ge(h_made, nrm + 1)
                    act.dma_start(table_tile(nrm), h_out[:, slot, :]).then_inc(h_stored[slot], 16)
                if "u" in stages:
                    place = upd % (2 * TILES_PER_GRAPH)
                    act.wait_ge(wh_ps_made, upd + 1)
                    act.activation(wh[:, bass.ds(place, 1), 0:CH], wh_ps[:, 0:CH], ACT.Copy)
                    act.activation(s1[:, bass.ds(place, 1)], wh_ps[:, CH:CH + 1], ACT.Copy)
                    act.activation(s2[:, bass.ds(place * P, P)], s2_ps, ACT.Copy).then_inc(s2_made, 1)
                if "a" in stages and late:
                    exponentials()

            run_steps(act, step)

        @block.tensor
        def _(pe):
            pe.wait_ge(pool_made, 23)
            pe.wait_ge(dve_consts_made, 3)

            def transpose_sign(tile):
                pe.wait_ge(nbr_made, tile + 1)
                for half in range(2):
                    wait(pe, nbr_t_made, (tile - 1) * 2 + half + 1)
                    for j in range(8):
                        col = (8 * half + j) * P
                        last = pe.transpose(nbr_ps[half][:, j, :], nbr_sign[:, col:col + P], ident_b[:])
                    last.then_inc(nbr_ps_made, 1)

            def pack_bytes(tile):
                wait(pe, vals_made, tile)
                pe.wait_ge(nbr_t_made, tile * 2 + 2)
                width = P // GROUP
                for j in range(TILES_PER_GRAPH):
                    last = pe.matmul(byte_ps[:, j * width:(j + 1) * width], is_nbr_t[:, j, :], byte_w[:],
                                     start=True, stop=True)
                last.then_inc(byte_made, 1)

            def step(k, slot, stages):
                upd, mul = k - UPDATE_LAG, k - MULTIPLY_LAG
                if at(k, 0):
                    transpose_sign(0)
                    pack_bytes(0)
                if at(k, UPDATE_LAG):
                    pe.wait_ge(weights_loaded, 64)
                    pe.wait_ge(dve_consts_made, 8)
                def transpose_chunk(q):
                    wait(pe, pt_made, mul * CHUNKS + q - 1)
                    for j in range(4):
                        col = (4 * q + j) * P
                        last = pe.transpose(pt_ps[q % 2][:, j, :], e[:, 1 - slot, col:col + P], ident[:])
                    last.then_inc(pt_ps_made, 1)

                def multiply_chunk(q):
                    pe.wait_ge(pt_made, mul * CHUNKS + q + 1)
                    for j in range(4):
                        node_tile = 4 * q + j
                        place = mul // TILES_PER_GRAPH % 2 * TILES_PER_GRAPH + node_tile
                        last = pe.matmul(att_ps[:, 0:CH + 1], prob_t[:, q, j, :], wh[:, bass.ds(place, 1), :],
                                         start=node_tile == 0, stop=node_tile == TILES_PER_GRAPH - 1)
                    if q == CHUNKS - 1:
                        last.then_inc(att_made, 1)

                if "m" in stages:
                    pe.wait_ge(prob_made, mul + 1)
                    transpose_chunk(0)
                    transpose_chunk(1)
                if "u" in stages:
                    wait(pe, s2_made, upd)
                    pe.wait_ge(h_upd_loaded[slot], in_slot(upd, slot) * 16)
                    pe.wait_ge(agg_made, upd + 1)
                    for j in range(4):
                        half = (h_upd[:, slot, :] if j < 2 else agg[:])[:, j % 2 * P:(j % 2 + 1) * P]
                        last = pe.transpose(update_ps[:, j * P:(j + 1) * P], half, ident[:])
                    last.then_inc(ha_ps_made, 1)
                    pe.wait_ge(ha_t_made, upd + 1)
                    for j in range(4):
                        pe.matmul(y_ps, ha_t[:, j, :], w0_sb[:, j, :], start=j == 0, stop=False)
                    pe.matmul(y_ps, ones[0:1, :], b0_sb[:], start=False, stop=True).then_inc(y_made, 1)
                if "m" in stages:
                    transpose_chunk(2)
                    wait(pe, result_made, mul)
                    multiply_chunk(0)
                    transpose_chunk(3)
                if "b" in stages:
                    transpose_sign(k + 1)

                def update_end():
                    pe.wait_ge(h2_made, upd + 1)
                    for j in range(2):
                        last = pe.transpose(update_ps[:, j * P:(j + 1) * P], h2[:, j * P:(j + 1) * P], ident[:])
                    last.then_inc(h2_ps_made, 1)
                    pe.wait_ge(h2_t_made, upd + 1)
                    for j in range(2):
                        pe.matmul(wh_ps, h2_t[:, j, :], w1s[:, j, :], start=j == 0, stop=j == 1)
                    for j in range(2):
                        last = pe.matmul(s2_ps, w2_bc[:, j, :], h2_t[:, j, :], start=j == 0, stop=j == 1)
                    last.then_inc(wh_ps_made, 1)

                if "u" in stages and "p" not in stages:
                    update_end()
                if "m" in stages:
                    multiply_chunk(1)
                    multiply_chunk(2)
                if "b" in stages:
                    pack_bytes(k + 1)
                if "m" in stages:
                    multiply_chunk(3)
                if "u" in stages and "p" in stages:
                    update_end()

            run_steps(pe, step)


_INS = ["x", "adj", "L0_gnn_W", "L0_gnn_b", "L1_gnn_W", "L1_gnn_a"]


def kernel(**inputs):
    import numpy as np
    import concourse.bacc as bacc
    from concourse.bass_utils import run_bass_kernel_spmd

    nc = bacc.Bacc("TRN2", target_bir_lowering=False, num_devices=1)
    arrays, args = {}, []
    for name in _INS:
        array = np.ascontiguousarray(inputs[name])
        arrays[name] = array
        args.append(nc.dram_tensor(name, array.shape, mybir.dt.from_np(array.dtype), kind="ExternalInput").ap())
    out = nc.dram_tensor("out", (GRAPHS, NODES, CH), mybir.dt.float32, kind="ExternalOutput").ap()
    graph_layers(nc, *args, out)
    ran = run_bass_kernel_spmd(nc, [arrays], core_ids=[0])
    return ran.results[0]["out"]
```
